# Optimizing a Trainium2 kernel written in Bass

```python
import numpy as np
import jax
import jax.numpy as jnp

def _softmax(x, axis=-1):
    return jax.nn.softmax(x, axis=axis)

def _gelu(x):
    return jax.nn.gelu(x, approximate=True)

def _silu(x):
    return jax.nn.silu(x)

def _sigmoid(x):
    return jax.nn.sigmoid(x)

def _layernorm(x, axis=-1, eps=1e-05):
    m = jnp.mean(x, axis=axis, keepdims=True)
    v = jnp.var(x, axis=axis, keepdims=True)
    return (x - m) / jnp.sqrt(v + eps)

def _scatter_add(tgt, idx, src, axis=0):
    return tgt.at[idx].add(src)

def _segment_sum(src, seg, n):
    return jax.ops.segment_sum(src, seg, n)
kernel_name = 'mk_cond_resid_d4_seqx_r8_130fcc'

def setup_inputs(seed: int=0):
    np.random.seed(seed)
    _w = jnp.asarray

    def _rec_inputs():
        import jax
        import jax.numpy as jnp
        _rk = jax.random.key(seed)
        x = -0.0003929 + 0.9999 * jax.random.normal(jax.random.fold_in(_rk, 1), (128, 32, 512), jnp.float32)
        _lenS = 32 - jax.random.randint(jax.random.fold_in(_rk, 7), (128,), 0, max(1, 32 // 4) + 1, jnp.int32)
        _lenS2 = 32 - jax.random.randint(jax.random.fold_in(_rk, 8), (128,), 0, max(1, 32 // 4) + 1, jnp.int32)
        itok_B_78_3631 = jax.random.randint(jax.random.fold_in(_rk, 11), (128,), 78, 454, jnp.int32)
        itok_B_0_15 = jax.random.randint(jax.random.fold_in(_rk, 12), (128,), 0, 16, jnp.int32)
        itok_B_2_6 = jax.random.randint(jax.random.fold_in(_rk, 13), (128,), 2, 7, jnp.int32)
        return (x, itok_B_78_3631, itok_B_0_15, itok_B_2_6)
    x, itok_B_78_3631, itok_B_0_15, itok_B_2_6 = _rec_inputs()

    def _L0_cond_setup():
        import math
        import jax, jax.numpy as jnp
        import numpy as np
        B, H, N, L = (16, 32, 64, 512)
        DT_MIN, DT_MAX = (0.001, 0.1)

        def _get_kernel(log_dt, C, log_A_real, A_imag, length):
            dt = jnp.exp(log_dt)
            Cc = C[..., 0] + 1j * C[..., 1]
            A = -jnp.exp(log_A_real) + 1j * A_imag
            dtA = A * dt[:, None]
            Ct = Cc * (jnp.exp(dtA) - 1.0) / A
            P = dtA[:, :, None] * jnp.arange(length, dtype=jnp.float32)
            K = 2.0 * jnp.einsum('hn,hnl->hl', Ct, jnp.exp(P)).real
            return K
        key = jax.random.key(seed)
        ks = jax.random.split(key, 5)
        u = jax.random.normal(ks[0], (B, H, L), dtype=jnp.float32)
        log_dt = jax.random.uniform(ks[1], (H,), dtype=jnp.float32) * (math.log(DT_MAX) - math.log(DT_MIN)) + math.log(DT_MIN)
        C = jax.random.normal(ks[2], (H, N, 2), dtype=jnp.float32)
        log_A_real = jnp.log(0.5 * jnp.ones((H, N), dtype=jnp.float32))
        A_imag = math.pi * jnp.broadcast_to(jnp.arange(N, dtype=jnp.float32), (H, N))
        D = jax.random.normal(ks[3], (H,), dtype=jnp.float32)
        length = jax.random.randint(ks[4], (B,), 1, L + 1, dtype=jnp.int32)
        return {'u': u, 'log_dt': log_dt, 'C': C, 'log_A_real': log_A_real, 'A_imag': A_imag, 'D': D, 'length': length}
    _L0_cond_all = _L0_cond_setup()
    _L0_cond_in = {k: v for k, v in _L0_cond_all.items() if k in ('log_dt', 'C', 'log_A_real', 'A_imag', 'D')}
    del _L0_cond_all

    def _L1_cond_setup():
        import jax, jax.numpy as jnp
        import numpy as np
        B, C, T = (64, 32, 512)
        S, D = (16, 32)
        key = jax.random.key(seed)
        k1, k2, k3 = jax.random.split(key, 3)
        x = jax.random.normal(k1, (B, C, T), dtype=jnp.float32)
        condition = jax.random.randint(k2, (B,), 0, S, dtype=jnp.int64)
        bound = float(np.sqrt(6.0 / C))
        weights = jax.random.uniform(k3, (S, C, D), dtype=jnp.float32, minval=-bound, maxval=bound)
        return {'x': x, 'condition': condition, 'weights': weights}
    _L1_cond_all = _L1_cond_setup()
    _L1_cond_in = {k: v for k, v in _L1_cond_all.items() if k in ('weights',)}
    del _L1_cond_all

    def _L2_cond_setup():
        import jax, jax.numpy as jnp
        import numpy as np
        NUM_CONDITIONS = 16
        IN_CH = 32
        OUT_CH = 32
        B = 64
        T = 512
        key = jax.random.key(seed)
        k_x, k_w, k_c = jax.random.split(key, 3)
        x = jax.random.normal(k_x, (B, IN_CH, T), dtype=jnp.float32)
        bound = float(np.sqrt(6.0 / IN_CH))
        weights = jax.random.uniform(k_w, (NUM_CONDITIONS, IN_CH, OUT_CH), dtype=jnp.float32, minval=-bound, maxval=bound)
        condition = jax.random.randint(k_c, (B,), 0, NUM_CONDITIONS, dtype=jnp.int64)
        return {'x': x, 'weights': weights, 'condition': condition}
    _L2_cond_all = _L2_cond_setup()
    _L2_cond_in = {k: v for k, v in _L2_cond_all.items() if k in ('weights',)}
    del _L2_cond_all

    def _L3_cond_setup():
        import jax, jax.numpy as jnp
        import numpy as np
        B, N, H, F = (4, 64, 512, 1376)
        L, R, RANK = (1, 16, 16)
        SCALE = 0.5
        key = jax.random.key(seed)
        ks = jax.random.split(key, 12)
        nrm = lambda k, shape, fan: jax.random.normal(k, shape, jnp.float32) * fan ** (-0.5)
        inp = {'x': jax.random.normal(ks[0], (B, N, H), jnp.float32), 'W_gate': nrm(ks[1], (F, H), H), 'W_up': nrm(ks[2], (F, H), H), 'W_down': nrm(ks[3], (H, F), F), 'A_gate': nrm(ks[4], (L, R, RANK, H), H), 'B_gate': nrm(ks[5], (L, R, F, RANK), RANK), 'A_up': nrm(ks[6], (L, R, RANK, H), H), 'B_up': nrm(ks[7], (L, R, F, RANK), RANK), 'A_down': nrm(ks[8], (L, R, RANK, F), F), 'B_down': nrm(ks[9], (L, R, H, RANK), RANK), 'lora_indices': jax.random.randint(ks[10], (B,), 0, R), 'layer_idx': 0}
        return inp
    _L3_cond_all = _L3_cond_setup()
    _L3_cond_in = {k: v for k, v in _L3_cond_all.items() if k in ('W_gate', 'W_up', 'W_down', 'A_gate', 'B_gate', 'A_up', 'B_up', 'A_down', 'B_down')}
    del _L3_cond_all
    return {'x': x, 'itok_B_78_3631': itok_B_78_3631, 'itok_B_0_15': itok_B_0_15, 'itok_B_2_6': itok_B_2_6, 'L0_cond_log_dt': _L0_cond_in['log_dt'], 'L0_cond_C': _L0_cond_in['C'], 'L0_cond_log_A_real': _L0_cond_in['log_A_real'], 'L0_cond_A_imag': _L0_cond_in['A_imag'], 'L0_cond_D': _L0_cond_in['D'], 'L1_cond_weights': _L1_cond_in['weights'], 'L2_cond_weights': _L2_cond_in['weights'], 'L3_cond_W_gate': _L3_cond_in['W_gate'], 'L3_cond_W_up': _L3_cond_in['W_up'], 'L3_cond_W_down': _L3_cond_in['W_down'], 'L3_cond_A_gate': _L3_cond_in['A_gate'], 'L3_cond_B_gate': _L3_cond_in['B_gate'], 'L3_cond_A_up': _L3_cond_in['A_up'], 'L3_cond_B_up': _L3_cond_in['B_up'], 'L3_cond_A_down': _L3_cond_in['A_down'], 'L3_cond_B_down': _L3_cond_in['B_down']}

def reference(x, itok_B_78_3631, itok_B_0_15, itok_B_2_6, L0_cond_log_dt, L0_cond_C, L0_cond_log_A_real, L0_cond_A_imag, L0_cond_D, L1_cond_weights, L2_cond_weights, L3_cond_W_gate, L3_cond_W_up, L3_cond_W_down, L3_cond_A_gate, L3_cond_B_gate, L3_cond_A_up, L3_cond_B_up, L3_cond_A_down, L3_cond_B_down):
    import jax
    import jax.numpy as jnp

    def _L0_cond_ref(u, log_dt, C, log_A_real, A_imag, D, length):
        import math
        import jax, jax.numpy as jnp
        import numpy as np
        B, H, N, L = (16, 32, 64, 512)
        DT_MIN, DT_MAX = (0.001, 0.1)

        def _get_kernel(log_dt, C, log_A_real, A_imag, length):
            dt = jnp.exp(log_dt)
            Cc = C[..., 0] + 1j * C[..., 1]
            A = -jnp.exp(log_A_real) + 1j * A_imag
            dtA = A * dt[:, None]
            Ct = Cc * (jnp.exp(dtA) - 1.0) / A
            P = dtA[:, :, None] * jnp.arange(length, dtype=jnp.float32)
            K = 2.0 * jnp.einsum('hn,hnl->hl', Ct, jnp.exp(P)).real
            return K
        Bq, Hq, Lq = u.shape
        K = _get_kernel(log_dt, C, log_A_real, A_imag, Lq)
        n = 2 * Lq
        kf = jnp.fft.rfft(K, n=n)
        uf = jnp.fft.rfft(u, n=n)
        y = jnp.fft.irfft(uf * kf[None], n=n)[..., :Lq]
        y = y + u * D[:, None]
        mask = (jnp.arange(Lq)[None, :] < length[:, None]).astype(u.dtype)
        return y * mask[:, None, :]

    def _L1_cond_ref(x, condition, weights):
        import jax, jax.numpy as jnp
        import numpy as np
        B, C, T = (64, 32, 512)
        S, D = (16, 32)
        W = weights[condition]
        return jnp.einsum('bct,bcd->bdt', x, W)

    def _L2_cond_ref(x, weights, condition):
        import jax, jax.numpy as jnp
        import numpy as np
        NUM_CONDITIONS = 16
        IN_CH = 32
        OUT_CH = 32
        B = 64
        T = 512
        W = weights[condition]
        return jnp.einsum('bct,bcd->bdt', x, W)

    def _L3_cond_ref(x, W_gate, W_up, W_down, A_gate, B_gate, A_up, B_up, A_down, B_down, lora_indices, layer_idx):
        import jax, jax.numpy as jnp
        import numpy as np
        B, N, H, F = (4, 64, 512, 1376)
        L, R, RANK = (1, 16, 16)
        SCALE = 0.5

        def lora_add(base, inp, A, B):
            Ab = A[layer_idx][lora_indices]
            Bb = B[layer_idx][lora_indices]
            t = jnp.einsum('bri,bni->bnr', Ab, inp)
            return base + jnp.einsum('bor,bnr->bno', Bb, t) * SCALE
        gate = lora_add(jnp.einsum('bnh,fh->bnf', x, W_gate), x, A_gate, B_gate)
        up = lora_add(jnp.einsum('bnh,fh->bnf', x, W_up), x, A_up, B_up)
        act = jax.nn.silu(gate) * up
        down = lora_add(jnp.einsum('bnf,hf->bnh', act, W_down), act, A_down, B_down)
        return down
    x = x + _L0_cond_ref(x, L0_cond_log_dt, L0_cond_C, L0_cond_log_A_real, L0_cond_A_imag, L0_cond_D, itok_B_78_3631)
    x = x + _L1_cond_ref(x, itok_B_0_15, L1_cond_weights)
    x = x + _L2_cond_ref(x, L2_cond_weights, itok_B_0_15)
    x = x + _L3_cond_ref(x, L3_cond_W_gate, L3_cond_W_up, L3_cond_W_down, L3_cond_A_gate, L3_cond_B_gate, L3_cond_A_up, L3_cond_B_up, L3_cond_A_down, L3_cond_B_down, itok_B_2_6, 0)
    return x

_drawn_inputs = setup_inputs


def setup_inputs(seed=0):
    import zlib

    import numpy as np

    out = dict(_drawn_inputs(seed))
    spreads = {'L0_cond_log_A_real': (-0.6931471824645996, 0.2)}
    factors = {}
    for name, (base, spread) in spreads.items():
        noise = np.random.default_rng([zlib.crc32(name.encode()), seed]).standard_normal(out[name].shape)
        drawn = base * np.exp(spread * noise) if base else spread * noise
        out[name] = jnp.asarray(drawn.astype(out[name].dtype))
    for name, factor in factors.items():
        out[name] = (out[name] * factor).astype(out[name].dtype)
    return out
```

```python
import math
from contextlib import ExitStack

import concourse.bass as bass
from concourse import mybir

ALU = mybir.AluOpType
ACT = mybir.ActivationFunctionType
F32 = mybir.dt.float32
F32R = mybir.dt.float32r
I32 = mybir.dt.int32

B, C, T = 128, 32, 512
NS = 64
NCOND = 16
F = 1376
NA, RANK = 16, 16
P = 128
KT = T // P
FT = -(-F // P)
FTAIL = F - (FT - 1) * P
FP = FT * P
UI, UN = 32, T // 32
GB = P // C
NG = 2
BB = NG * GB
TB = BB * C
NBLK = B // BB
WC = 704
WGU = 2 * KT * FP
WCOLS = WGU + FT * T
NWC = WCOLS // WC
BJ = 2
BCH = [list(range(j, min(j + BJ, FT))) for j in range(0, FT, BJ)]
WA, WAD, WB, WBD = 2 * KT * RANK, FT * RANK, FT * 2 * P, T
ROUND = 12582912.0
PIC = 3.1415925
C1 = 6.28125
C2 = 1.93500518798828125e-3
C3 = 2.0 * math.pi - C1 - C2
K_ID, K_BLK, K_T, K_PU, K_PV, K_S = 0, 128, 256, 768, 784, 816
K_N = 820
UCOLS, VCOLS = C * UN, C * UI
X_SB = UCOLS
X_SBH = UCOLS + C
X_COS = UCOLS + 2 * C
X_CB = X_COS + UCOLS
X_V = X_CB + C
X_N = X_V + VCOLS


def cond_resid_kernel(nc, xT, x, lens, cidx, lidx, ssm, dskip, cst, w1t, w2, wall, ta, tad, tb, tbd, out):
    kpad = nc.dram_tensor("kpad", (C, P + T), F32, kind="Internal").ap()
    x1p = nc.dram_tensor("x1p", (B * C, T), F32, kind="Internal").ap()
    tm_d = nc.dram_tensor("tm_d", (NCOND, C, 2, C), F32, kind="Internal").ap()
    ta_d = nc.dram_tensor("ta_d", (NA, P, 2, WA), F32, kind="Internal").ap()
    tad_d = nc.dram_tensor("tad_d", (NA, P, 2, WAD), F32, kind="Internal").ap()
    tb_d = nc.dram_tensor("tb_d", (NA, 2 * RANK, WB), F32, kind="Internal").ap()
    tbd_d = nc.dram_tensor("tbd_d", (NA, 2 * RANK, WBD), F32, kind="Internal").ap()
    x1p_bct = x1p.rearrange("(b c) t -> b c t", c=C)

    ctx = ExitStack()
    with ctx:
        def sem(name):
            return ctx.enter_context(nc.semaphore(name))

        def sbin(stack):
            return lambda name, shape, dt=F32: stack.enter_context(nc.sbuf_tensor(name, shape, dt))

        ps = ctx.enter_context(nc.psum_tensor("ps", [P, 8, 512], F32))
        acc = [ps[:, g, :] for g in range(NG)]
        x3p = [ps[:, 2 + g, :] for g in range(NG)]
        wk = [ps[:, 4 + n, :] for n in range(2)]
        la = ps[:, 6, :]
        tdp = ps[:, 7, :]
        yp = [ps[:, n, :] for n in range(4)]
        kp = [ps[0:UN, 6 + n, :] for n in range(2)]
        wmp = ps[0:C, 5, :]

        sb = sbin(ctx)
        cs = sb("cs", [P, K_N])
        ixs = sb("ixs", [1, 2 * B], I32)
        prep = ExitStack()
        sb = sbin(prep)
        pk = sb("pk", [P, 5, C])
        dsk = sb("dsk", [1, C])
        xs = sb("xs", [P, X_N])
        kk = sb("kk", [P, X_N])
        ex = sb("ex", [P, UCOLS + VCOLS])
        sm = sb("sm", [P, 24, C])
        wtmp = sb("wtmp", [P, 2, UCOLS])
        zer = sb("zer", [C, P])
        kf = sb("kf", [UN, C, UI])
        w1s = sb("w1s", [C, NCOND, C])
        w2s = sb("w2s", [C, NCOND, C])
        wms = sb("wms", [C, NCOND, 2, C])
        ta_r = sb("ta_r", [P, NA, WA])
        tad_r = sb("tad_r", [P, NA, WAD])
        tb_r = sb("tb_r", [P, 2, WB])
        tbd_r = sb("tbd_r", [P, 2, WBD])
        ta_h = sb("ta_h", [P, NA, WA])
        tad_h = sb("tad_h", [P, NA, WAD])
        tb_h = sb("tb_h", [P, WB])
        tbd_h = sb("tbd_h", [P, 2, WBD])
        prep.close()
        sb = sbin(ctx)
        wres = [sb("w_hi", [P, WCOLS], F32R), sb("w_lo", [P, WCOLS], F32R)]
        conv = ExitStack()
        sb = sbin(conv)
        ur = sb("ur", [P, 4, KT * B])
        tr = sb("tr", [P, 4, T])
        us = [sb("us_hi", [P, 2, KT * B], F32R), sb("us_lo", [P, 2, KT * B], F32R)]
        ts_ = [sb("ts_hi", [P, 2, T], F32R), sb("ts_lo", [P, 2, T], F32R)]
        yo = sb("yo", [P, 2, T])
        wr = sb("wr", [P, 3, WC])
        mk = sb("mk", [P, T])
        leni = sb("leni", [P, 1], I32)
        lenf = sb("lenf", [P, 1])
        conv.close()
        sb = sbin(ctx)
        ag = sb("ag", [P, BB, 2, WA], F32R)
        adg = sb("adg", [P, BB, 2, WAD], F32R)
        bg = sb("bg", [P, 2, NG, BJ, 2, P], F32R)
        bdg = sb("bdg", [P, NG, WBD], F32R)
        x1s = [sb("x1_hi", [P, NG, T], F32R), sb("x1_lo", [P, NG, T], F32R)]
        io = sb("io", [P, 2, T])
        wbd = sb("wbd", [P, NG, 2, P], F32R)
        x3s = [sb("x3_hi", [P, KT, TB], F32R), sb("x3_lo", [P, KT, TB], F32R)]
        tsb = sb("tsb", [P, NG * 2 * P])
        th = [sb("t_hi", [P, NG, 2, P], F32R), sb("t_lo", [P, NG, 2, P], F32R)]
        sg = sb("sg", [P, 2, TB])
        ac = [sb("act_hi", [P, 2, TB], F32R), sb("act_lo", [P, 2, TB], F32R)]
        tdm = sb("tdm", [P, NG * P])
        tdd = sb("tdd", [P, NG, P])
        tdt = [sb("tdt_hi", [P, NG, P], F32R), sb("tdt_lo", [P, NG, P], F32R)]

        names = """pk cst small lens tabs w12 zer kf kst kout wm wms tst u0 u1 u2 u3 tt0 tt1 tt2 tt3 wl0 wl1 wl2
            a1 dch ph ex tg kuv kps uhi thi usp0 usp1 usp2 usp3 tsp0 tsp1 tsp2 tsp3 whi wsp0 wsp1 wsp2 y0 y1
            ev0 ev1 ev2 ev3 yst0 yst1 mask done tah tal tbh tbl tbs prepped
            tt ag adg b0 b1 bdg wbd xin xsum x1hi x1lo x3mm x3hi x3lo la tm th tl gu silu mul ahi alo down accin
            tdone tdm tdd tdx tdth tdtl accd accA accD ost wz""".split()
        s = {n: sem("s_" + n) for n in names}

        def at(eng, value):
            return value if isinstance(value, int) else eng.snap(value)

        wgu = [w[:, 0:WGU].rearrange("p (u k f) -> p u k f", u=2, k=KT) for w in wres]
        wdn = [w[:, WGU:WCOLS].rearrange("p (j t) -> p j t", j=FT) for w in wres]
        ident = cs[:, K_ID:K_ID + P]
        blk = cs[:, K_BLK:K_BLK + P]
        tvals = cs[:, K_T:K_T + T]

        block = ctx.enter_context(nc.Block())

        @block.sync
        def _(sp):
            sp.dma_start(pk[:], ssm).then_inc(s["pk"], 16)
            sp.dma_start(cs[:], cst).then_inc(s["cst"], 16)
            sp.dma_start(w1s[:], w1t).then_inc(s["w12"], 16)
            sp.dma_start(w2s[:], w2).then_inc(s["w12"], 16)
            sp.dma_start(dsk[:], dskip).then_inc(s["small"], 16)
            sp.dma_start(leni[:], lens).then_inc(s["lens"], 16)
            sp.dma_start(ixs[:, 0:B], lidx).then_inc(s["small"], 16)
            sp.dma_start(ixs[:, B:2 * B], cidx).then_inc(s["small"], 16)
            for k in range(4):
                sp.dma_start(ur[:, k, :], xT[k]).then_inc(s[f"u{k}"], 16)
            sp.dma_start(tb_r[:, 0, :], tb[0]).then_inc(s["tabs"], 16)
            sp.wait_ge(s["tabs"], 16)
            sp.dma_start(tb_r[:, 1, :], tb[1]).then_inc(s["tabs"], 16)
            sp.wait_ge(s["tabs"], 32)
            sp.dma_start(ta_r[:], ta).then_inc(s["tabs"], 16)
            sp.wait_ge(s["tabs"], 48)
            sp.dma_start(tad_r[:], tad).then_inc(s["tabs"], 16)
            sp.wait_ge(s["tabs"], 64)
            sp.dma_start(tbd_r[:], tbd).then_inc(s["tabs"], 16)
            sp.wait_ge(s["zer"], 1)
            sp.dma_start(kpad[:, 0:P - 1], zer[:, 0:P - 1]).then_inc(s["kout"], 16)
            sp.wait_ge(s["kf"], 1)
            sp.dma_start(kpad[:, P - 1:P - 1 + T].rearrange("h (i j) -> i h j", j=UI), kf[:]).then_inc(s["kout"], 16)
            sp.wait_ge(s["kout"], 32)

            def load_toeplitz(h, k):
                src = bass.AP(kpad.tensor, h * (P + T), [[1, P], [1, T]])
                sp.dma_start(tr[:, k, :], src).then_inc(s[f"tt{k}"], 16)

            for k in range(4):
                load_toeplitz(k, k)
            sp.wait_ge(s["wms"], 2)
            sp.dma_start(tm_d.rearrange("s c l d -> c s l d"), wms[:]).then_inc(s["tst"], 16)
            npr = P // RANK
            for n in range(2):
                sp.wait_ge(s["tah"], n + 1)
                for r in range(npr):
                    sp.dma_start(tb_d[n * npr + r, 0:RANK, :],
                                 tb_h[r * RANK:(r + 1) * RANK, :]).then_inc(s["tbs"], 16)
                sp.wait_ge(s["tal"], n + 1)
                for r in range(npr):
                    sp.dma_start(tb_d[n * npr + r, RANK:2 * RANK, :],
                                 tb_r[r * RANK:(r + 1) * RANK, n, :]).then_inc(s["tst"], 16)
            for n, (dst, hi, lo) in enumerate(((ta_d, ta_h, ta_r), (tad_d, tad_h, tad_r))):
                for half, src, g in ((0, hi, "tah"), (1, lo, "tal")):
                    sp.wait_ge(s[g], 3 + n)
                    sp.dma_start(dst[:, :, half, :].rearrange("r p w -> p r w"),
                                 src[:]).then_inc(s["tst"], 16)
            for half, src, g in ((0, tbd_h, "tah"), (1, tbd_r, "tal")):
                sp.wait_ge(s[g], 5)
                for n in range(2):
                    for r in range(npr):
                        sp.dma_start(tbd_d[n * npr + r, half * RANK:(half + 1) * RANK, :],
                                     src[r * RANK:(r + 1) * RANK, n, :]).then_inc(s["tst"], 16)
            for q in range(3):
                sp.dma_start(wr[:, q, :], wall[:, q * WC:(q + 1) * WC]).then_inc(s[f"wl{q}"], 16)

            def conv_io(it, last):
                here = [at(sp, it * 4 + k) for k in range(4)]
                later = [at(sp, it * 4 + k + 4) for k in range(4)]
                chunk = [at(sp, (it * 3 + q + 3) * WC) for q in range(3)]
                for k in range(4):
                    m, n = k % 2, it * 2 + k // 2
                    sp.wait_ge(s[f"ev{k}"], it + 1)
                    sp.dma_start(x1p_bct[:, bass.ds(here[k], 1), :].rearrange("b c t -> b (c t)"),
                                 yo[:, m, :]).then_inc(s[f"yst{m}"], 16)
                    if not last:
                        sp.wait_ge(s[f"usp{k}"], it + 1)
                        sp.dma_start(ur[:, k, :], xT[bass.ds(later[k], 1)].rearrange("c p w -> p (c w)")
                                     ).then_inc(s[f"u{k}"], 16)
                        sp.wait_ge(s[f"tsp{k}"], it + 1)
                        load_toeplitz(later[k], k)
                    if k < 3 and not last:
                        sp.wait_ge(s[f"wsp{k}"], it + 1)
                        sp.dma_start(wr[:, k, :], wall[:, bass.ds(chunk[k], WC)]
                                     ).then_inc(s[f"wl{k}"], 16)

            with sp.Fori(0, C // 4 - 1) as it:
                conv_io(it, False)
            conv_io(C // 4 - 1, True)
            NST = 1 + 2 * npr + 4 + 4 * npr
            sp.wait_ge(s["tst"], 16 * NST)
            sp.wait_ge(s["tbs"], 16 * 2 * npr)
            sp.wait_ge(s["yst0"], 16 * C // 2)
            sp.wait_ge(s["yst1"], 16 * C // 2)
            sp.wait_ge(s["done"], 3)
            sp.wait_ge(s["wz"], 1)

            def rows_of(b):
                return b // GB, (b % GB) * C, (b % GB + 1) * C

            def gather(i, free, column, entries, dma, stored=None):
                for b in range(BB):
                    e = sp.value_load(ixs[0:1, bass.ds(i * BB + b + column, 1)], min_val=0, max_val=entries - 1)
                    if b == 0 and free is not None:
                        sp.wait_ge(*free)
                    if b == 1 and stored is not None:
                        sp.wait_ge(s["ost"], stored)
                    dma(b, bass.ds(e, 1))

            def load_ag(i, free):
                gather(i, free, 0, NA, lambda b, e: sp.dma_start(
                    ag[:, b, :, :].bitcast(F32), ta_d[e].rearrange("a p l w -> (a p) l w")).then_inc(s["ag"], 16))

            def load_adg(i, free):
                gather(i, free, 0, NA, lambda b, e: sp.dma_start(
                    adg[:, b, :, :].bitcast(F32), tad_d[e].rearrange("a p l w -> (a p) l w")).then_inc(s["adg"], 16))

            def load_b(i, c, free):
                o, w = BCH[c][0] * 2 * P, len(BCH[c]) * 2 * P

                def dma(b, e):
                    g, p0, p1 = rows_of(b)
                    sp.dma_start(bg[p0:p1, c % 2, g, :, :, :].rearrange("p j u f -> p (j u f)")[:, 0:w].bitcast(F32),
                                 tb_d[e, :, o:o + w].rearrange("a k w -> (a k) w")).then_inc(s[f"b{c % 2}"], 16)
                gather(i, free, 0, NA, dma)

            def load_bdg(i, free):
                def dma(b, e):
                    g, p0, p1 = rows_of(b)
                    sp.dma_start(bdg[p0:p1, g, :].bitcast(F32), tbd_d[e].rearrange("a k w -> (a k) w")
                                 ).then_inc(s["bdg"], 16)
                gather(i, free, 0, NA, dma)

            def load_x(i, free, stored):
                def dma(b, e):
                    g, p0, p1 = rows_of(b)
                    sp.dma_start(wbd[p0:p1, g, :, p0:p1].bitcast(F32), tm_d[e].rearrange("a c l d -> (a c) l d")
                                 ).then_inc(s["wbd"], 16)
                gather(i, free, B, NCOND, dma, stored)
                first = [at(sp, i * TB + g * P) for g in range(NG)]
                split = [at(sp, i * NG + g) for g in range(NG)]
                for g in range(NG):
                    sp.wait_ge(s["x1lo"], split[g])
                    rows = bass.ds(first[g], P)
                    sp.dma_start(io[:, 0, :], x1p[rows, :]).then_inc(s["xin"], 16)
                    sp.dma_start(io[:, 1, :], x[rows, :]).then_inc(s["xin"], 16)

            sp.sem_inc(s["ost"], 16)
            load_x(0, None, None)
            load_ag(0, None)
            load_b(0, 0, None)
            load_b(0, 1, None)
            load_adg(0, None)
            load_bdg(0, None)

            def block_io(i, last):
                if not last:
                    load_ag(i + 1, (s["la"], i + 1))
                    load_x(i + 1, (s["accin"], i + 1), i * 16 * NG + 16)
                for c in range(2, len(BCH) + 2):
                    free = (s["gu"], i * FT + BCH[c - 2][-1] + 1)
                    if c < len(BCH):
                        load_b(i, c, free)
                    elif not last:
                        load_b(i + 1, c - len(BCH), free)
                if not last:
                    load_adg(i + 1, (s["tdone"], i + 1))
                    load_bdg(i + 1, (s["accd"], i + 1))
                first = [at(sp, i * TB + g * P) for g in range(NG)]
                for g, name in enumerate(("accA", "accD")):
                    sp.wait_ge(s[name], i + 2)
                    sp.dma_start(out[bass.ds(first[g], P), :], io[:, g, :]).then_inc(s["ost"], 16)

            with sp.Fori(0, NBLK - 1) as i:
                block_io(i, False)
            block_io(NBLK - 1, True)
            sp.wait_ge(s["ost"], 16 * NG * NBLK + 16)

        @block.gpsimd
        def _(pool):
            nc.gpsimd.memset(zer[:], 0.0).then_inc(s["zer"], 1)
            tabs = ((tb_h[:], tb_r[:, 0, :], 1), (tb_h[:], tb_r[:, 1, :], 2), (ta_h[:], ta_r[:], 3),
                    (tad_h[:], tad_r[:], 4), (tbd_h[:], tbd_r[:], 5))
            for n, (hi, raw, _) in enumerate(tabs):
                pool.wait_ge(s["tah"], n + 1)
                nc.gpsimd.tensor_tensor(raw.bitcast(F32R), raw, hi, ALU.subtract).then_inc(s["tal"], 1)

            def lows(it):
                for k in range(4):
                    m = k % 2
                    pool.wait_ge(s["uhi"], it * 4 + k + 1)
                    nc.gpsimd.tensor_tensor(us[1][:, m, :], ur[:, k, :], us[0][:, m, :].bitcast(F32),
                                            ALU.subtract).then_inc(s[f"usp{k}"], 1)
                    pool.wait_ge(s["thi"], it * 4 + k + 1)
                    nc.gpsimd.tensor_tensor(ts_[1][:, m, :], tr[:, k, :], ts_[0][:, m, :].bitcast(F32),
                                            ALU.subtract).then_inc(s[f"tsp{k}"], 1)

            with pool.Fori(0, C // 4) as it:
                lows(it)
            pool.wait_ge(s["done"], 2)
            pool.wait_ge(s["yst0"], 16 * C // 2)
            pool.wait_ge(s["yst1"], 16 * C // 2)
            nc.gpsimd.memset(wbd[:].bitcast(F32), 0.0).then_inc(s["wz"], 1)
            pool.wait_ge(s["wz"], 1)
            pool.sem_inc(s["done"], 1)

            def block_sums(i):
                for g in range(NG):
                    pool.wait_ge(s["xin"], (i * NG + g + 1) * 32)
                    nc.gpsimd.tensor_tensor(io[:, 0, :], io[:, 0, :], io[:, 1, :], ALU.add).then_inc(s["xsum"], 1)
                    pool.wait_ge(s["x1hi"], i * NG + g + 1)
                    nc.gpsimd.tensor_tensor(x1s[1][:, g, :], io[:, 0, :], x1s[0][:, g, :].bitcast(F32),
                                            ALU.subtract).then_inc(s["x1lo"], 1)

            block_sums(0)

            def lows3(i, last):
                for j in range(FT):
                    m = P if j < FT - 1 else FTAIL
                    pool.wait_ge(s["ahi"], i * FT + j + 1)
                    nc.gpsimd.tensor_tensor(ac[1][0:m, j % 2, :], sg[0:m, j % 2, :], ac[0][0:m, j % 2, :].bitcast(F32),
                                            ALU.subtract).then_inc(s["alo"], 1)
                    if j == 2 and not last:
                        block_sums(i + 1)

            with pool.Fori(0, NBLK - 1) as i:
                lows3(i, False)
            lows3(NBLK - 1, True)

        @block.scalar
        def _(act):
            act.wait_ge(s["pk"], 16)
            nc.scalar.activation(sm[:, 0, :], pk[:, 4, :], ACT.Exp).then_inc(s["a1"], 1)
            nc.scalar.activation(sm[:, 1, :], pk[:, 0, :], ACT.Exp).then_inc(s["a1"], 1)
            act.wait_ge(s["ex"], 1)
            nc.scalar.activation(sm[:, 4, :], sm[:, 2, :], ACT.Tanh, scale=0.5).then_inc(s["a1"], 1)
            nc.scalar.activation(ex[:], ex[:], ACT.Exp).then_inc(s["a1"], 1)
            act.wait_ge(s["ph"], 1)
            nc.scalar.activation(xs[:], xs[:], ACT.Sin).then_inc(s["tg"], 1)
            act.wait_ge(s["wm"], 1)
            wm3 = wmp.rearrange("c (s d) -> c s d", d=C)
            nc.scalar.activation(wms[:, :, 0, :].bitcast(F32R), wm3, ACT.Copy).then_inc(s["wms"], 1)
            for n, (hi, raw) in enumerate(((tb_h[:], tb_r[:, 0, :]), (tb_h[:], tb_r[:, 1, :]), (ta_h[:], ta_r[:]),
                                           (tad_h[:], tad_r[:]), (tbd_h[:], tbd_r[:]))):
                act.wait_ge(s["tabs"], 16 * (n + 1))
                if n == 1:
                    act.wait_ge(s["tbs"], 16 * (P // RANK))
                    act.wait_ge(s["tal"], 1)
                nc.scalar.activation(hi.bitcast(F32R), raw, ACT.Copy).then_inc(s["tah"], 1)
            NST = 1 + 2 * (P // RANK) + 4 + 4 * (P // RANK)

            def highs(it, first):
                for k in range(4):
                    m, n = k % 2, it * 2 + k // 2
                    act.wait_ge(s[f"u{k}"], it * 16 + 16)
                    act.wait_ge(s[f"y{m}"], n)
                    nc.scalar.activation(us[0][:, m, :], ur[:, k, :], ACT.Copy).then_inc(s["uhi"], 1)
                    act.wait_ge(s[f"tt{k}"], it * 16 + 16)
                    nc.scalar.activation(ts_[0][:, m, :], tr[:, k, :], ACT.Copy).then_inc(s["thi"], 1)
                    if first and k == 1:
                        act.wait_ge(s["tst"], 16 * NST)
                        act.wait_ge(s["tbs"], 32 * (P // RANK))
                        act.wait_ge(s["kout"], 32)
                    if k >= 1:
                        q = k - 1
                        act.wait_ge(s[f"wl{q}"], it * 16 + 16)
                        nc.scalar.activation(wres[0][:, bass.ds((it * 3 + q) * WC, WC)], wr[:, q, :],
                                             ACT.Copy).then_inc(s["whi"], 1)

            highs(0, True)
            with act.Fori(1, C // 4) as it:
                highs(it, False)
            act.wait_ge(s["y0"], C // 2)
            act.wait_ge(s["y1"], C // 2)
            act.sem_inc(s["done"], 1)
            act.wait_ge(s["done"], 3)
            act.sem_inc(s["accA"], 1)

            def x1_hi(i):
                for g in range(NG):
                    act.wait_ge(s["xsum"], i * NG + g + 1)
                    nc.scalar.activation(x1s[0][:, g, :], io[:, 0, :], ACT.Copy).then_inc(s["x1hi"], 1)

            def x3_hi(i):
                for g in range(NG):
                    act.wait_ge(s["x3mm"], i * NG + g + 1)
                    nc.scalar.activation(x3s[0][:, :, g * P:(g + 1) * P],
                                         x3p[g].rearrange("p (k n) -> p k n", k=KT), ACT.Copy).then_inc(s["x3hi"], 1)

            def t_hi(i):
                act.wait_ge(s["tt"], i + 1)
                nc.scalar.activation(th[0][:].rearrange("p g u n -> p (g u n)"), la, ACT.Copy
                                     ).then_inc(s["th"], 1)

            def act_tile(i, j):
                m = P if j < FT - 1 else FTAIL
                act.wait_ge(s["gu"], i * FT + j + 1)
                nc.scalar.activation(sg[0:m, j % 2, :], wk[j % 2][0:m, 0:TB], ACT.Silu).then_inc(s["silu"], 1)
                act.wait_ge(s["mul"], i * FT + j + 1)
                nc.scalar.activation(ac[0][0:m, j % 2, :], sg[0:m, j % 2, :], ACT.Copy).then_inc(s["ahi"], 1)

            x1_hi(0)
            x3_hi(0)
            t_hi(0)
            act_tile(0, 0)

            def act_block(i, last):
                for j in range(1, FT):
                    act_tile(i, j)
                    if j == 2 and not last:
                        act.wait_ge(s["accin"], i + 1)
                        x1_hi(i + 1)
                if not last:
                    x3_hi(i + 1)
                    t_hi(i + 1)
                act.wait_ge(s["tdx"], i + 1)
                nc.scalar.activation(tdt[0][:].rearrange("p g n -> p (g n)"), tdp[:, 256:512], ACT.Copy
                                     ).then_inc(s["tdth"], 1)
                if not last:
                    act_tile(i + 1, 0)
                act.wait_ge(s["accd"], i + 1)
                nc.scalar.activation(io[:, 0, :], acc[0], ACT.Copy).then_inc(s["accA"], 1)

            with act.Fori(0, NBLK - 1) as i:
                act_block(i, False)
            act_block(NBLK - 1, True)

        @block.vector
        def _(dve):
            chain = [0]

            def link(ins):
                chain[0] += 1
                ins.then_inc(s["dch"], 1)
                dve.wait_ge(s["dch"], chain[0])

            V = nc.vector
            dve.wait_ge(s["a1"], 2)
            dve.wait_ge(s["cst"], 16)

            def v(n):
                return sm[:, n, :]

            DT, EA, A_, BI, TH = 0, 1, 2, 3, 4
            aim, cr, ci = pk[:, 1, :], pk[:, 2, :], pk[:, 3, :]
            link(V.scalar_tensor_tensor(out=v(A_), in0=v(EA), scalar=-1.0, in1=v(DT), op0=ALU.mult, op1=ALU.mult))
            link(V.tensor_tensor(v(BI), aim, v(DT), ALU.mult))
            pu = cs[:, K_PU:K_PU + UN]
            pv = cs[:, K_PV:K_PV + UI]

            def outer(dst, col, powers, n):
                return V.tensor_tensor(dst.rearrange("p (h n) -> p h n", n=n),
                                       v(col).unsqueeze(2).to_broadcast([P, C, n]),
                                       powers.unsqueeze(1).to_broadcast([P, C, n]), ALU.mult)

            outer(ex[:, 0:UCOLS], A_, pu, UN)
            outer(ex[:, UCOLS:], A_, pv, UI).then_inc(s["ex"], 1)
            outer(xs[:, 0:UCOLS], BI, pu, UN)
            outer(xs[:, X_COS:X_COS + UCOLS], BI, pu, UN)
            outer(xs[:, X_V:X_N], BI, pv, UI)
            V.tensor_copy(xs[:, X_SB:X_SB + C], v(BI))
            V.tensor_copy(xs[:, X_CB:X_CB + C], v(BI))
            link(V.tensor_scalar(xs[:, X_SBH:X_SBH + C], v(BI), 0.5, None, ALU.mult))
            i2p = 1.0 / (2.0 * math.pi)
            parts = ((0, X_COS, 0.0, 0.0), (X_COS, X_V, 0.25, math.pi / 2),
                     (X_V, X_N, cs[:, K_S + 2:K_S + 3], cs[:, K_S + 3:K_S + 4]))
            for lo, hi, turn, _ in parts:
                last = V.tensor_scalar(kk[:, lo:hi], xs[:, lo:hi], i2p, turn, ALU.mult, ALU.add)
            link(last)
            link(V.tensor_scalar(kk[:], kk[:], ROUND, None, ALU.add))
            link(V.tensor_scalar(kk[:], kk[:], -ROUND, None, ALU.add))
            for c in (C1, C2, C3):
                link(V.scalar_tensor_tensor(out=xs[:], in0=kk[:], scalar=-c, in1=xs[:], op0=ALU.mult, op1=ALU.add))
            for lo, hi, _, off in parts:
                last = V.tensor_scalar(xs[:, lo:hi], xs[:, lo:hi], off, PIC, ALU.add, ALU.min)
            link(last)
            V.tensor_scalar(xs[:], xs[:], -PIC, None, ALU.max).then_inc(s["ph"], 1)
            dve.wait_ge(s["w12"], 32)
            idc = cs[0:C, K_ID:K_ID + C].unsqueeze(1).to_broadcast([C, NCOND, C])
            V.tensor_tensor(w1s[:], w1s[:], idc, ALU.add)
            V.tensor_tensor(w2s[:], w2s[:], idc, ALU.add).then_inc(s["kst"], 1)
            dve.wait_ge(s["a1"], 4)
            OM, RC, EM, A2, I2, ER, EI, GR, GI, TR_, TI = 5, 6, 7, 8, 9, 10, 11, 12, 13, 14, 15
            T1, T2, PP, QQ = 16, 17, 18, 19
            link(V.tensor_scalar(v(OM), v(TH), -1.0, 1.0, ALU.mult, ALU.add))
            link(V.reciprocal(v(RC), v(OM)))
            link(V.scalar_tensor_tensor(out=v(EM), in0=v(TH), scalar=2.0, in1=v(RC), op0=ALU.mult, op1=ALU.mult))
            link(V.tensor_tensor(v(A2), v(EA), v(EA), ALU.mult))
            link(V.tensor_tensor(v(T1), aim, aim, ALU.mult))
            link(V.tensor_tensor(v(A2), v(A2), v(T1), ALU.add))
            link(V.reciprocal(v(I2), v(A2)))
            dve.wait_ge(s["tg"], 1)
            sb_, cb, sbh = xs[:, X_SB:X_SB + C], xs[:, X_CB:X_CB + C], xs[:, X_SBH:X_SBH + C]
            link(V.tensor_tensor(v(T1), sbh, sbh, ALU.mult))
            link(V.tensor_tensor(v(ER), v(EM), cb, ALU.mult))
            link(V.scalar_tensor_tensor(out=v(ER), in0=v(T1), scalar=-2.0, in1=v(ER), op0=ALU.mult, op1=ALU.add))
            link(V.scalar_tensor_tensor(out=v(EI), in0=v(EM), scalar=1.0, in1=sb_, op0=ALU.add, op1=ALU.mult))
            link(V.tensor_tensor(v(T1), v(EI), aim, ALU.mult))
            link(V.tensor_tensor(v(T2), v(ER), v(EA), ALU.mult))
            link(V.tensor_tensor(v(T1), v(T1), v(T2), ALU.subtract))
            link(V.tensor_tensor(v(GR), v(T1), v(I2), ALU.mult))
            link(V.tensor_tensor(v(T1), v(EI), v(EA), ALU.mult))
            link(V.tensor_tensor(v(T2), v(ER), aim, ALU.mult))
            link(V.tensor_tensor(v(T1), v(T1), v(T2), ALU.add))
            link(V.scalar_tensor_tensor(out=v(GI), in0=v(T1), scalar=-1.0, in1=v(I2), op0=ALU.mult, op1=ALU.mult))
            link(V.tensor_tensor(v(T1), cr, v(GR), ALU.mult))
            link(V.tensor_tensor(v(T2), ci, v(GI), ALU.mult))
            link(V.tensor_tensor(v(TR_), v(T1), v(T2), ALU.subtract))
            link(V.tensor_tensor(v(T1), cr, v(GI), ALU.mult))
            link(V.tensor_tensor(v(T2), ci, v(GR), ALU.mult))
            link(V.tensor_tensor(v(TI), v(T1), v(T2), ALU.add))
            sre, sim = cs[:, K_S:K_S + 1], cs[:, K_S + 1:K_S + 2]
            link(V.tensor_scalar(v(T1), v(TI), sim, None, ALU.mult))
            link(V.scalar_tensor_tensor(out=v(PP), in0=v(TR_), scalar=sre, in1=v(T1), op0=ALU.mult, op1=ALU.subtract))
            link(V.tensor_scalar(v(T2), v(TR_), sim, None, ALU.mult))
            link(V.scalar_tensor_tensor(out=v(QQ), in0=v(TI), scalar=sre, in1=v(T2), op0=ALU.mult, op1=ALU.add))
            us3, uc3 = wtmp[:, 0, :].rearrange("p (h n) -> p h n", n=UN), wtmp[:, 1, :].rearrange("p (h n) -> p h n", n=UN)
            V.tensor_tensor(us3, xs[:, 0:UCOLS].rearrange("p (h n) -> p h n", n=UN),
                            v(QQ).unsqueeze(2).to_broadcast([P, C, UN]), ALU.mult)
            link(V.tensor_tensor(uc3, xs[:, X_COS:X_COS + UCOLS].rearrange("p (h n) -> p h n", n=UN),
                                 v(PP).unsqueeze(2).to_broadcast([P, C, UN]), ALU.mult))
            link(V.tensor_tensor(wtmp[:, 0, :], wtmp[:, 1, :], wtmp[:, 0, :], ALU.subtract))
            V.tensor_tensor(wtmp[:, 0, :], wtmp[:, 0, :], ex[:, 0:UCOLS], ALU.mult)
            V.tensor_tensor(xs[:, X_V:X_N], xs[:, X_V:X_N], ex[:, UCOLS:], ALU.mult).then_inc(s["kuv"], 1)
            dve.wait_ge(s["wms"], 1)
            V.tensor_tensor(wms[:, :, 1, :].bitcast(F32R), wmp.rearrange("c (s d) -> c s d", d=C),
                            wms[:, :, 0, :], ALU.subtract).then_inc(s["wms"], 1)
            dve.wait_ge(s["kps"], 1)
            for n in range(2):
                last = V.tensor_scalar(kf[:].rearrange("i h j -> i (h j)")[:, n * 512:(n + 1) * 512], kp[n], 2.0,
                                       None, ALU.mult)
            link(last)
            dve.wait_ge(s["small"], 48)
            d0 = kf[0:1, :, 0:1].rearrange("i h j -> i (h j)")
            V.tensor_tensor(d0, d0, dsk[:], ALU.add).then_inc(s["kf"], 1)
            dve.wait_ge(s["lens"], 16)
            link(V.tensor_copy(lenf[:], leni[:]))
            link(V.tensor_scalar(mk[:], tvals, lenf[:, 0:1], None, ALU.is_lt))

            def evac(it):
                for k in range(4):
                    m, n = k % 2, it * 2 + k // 2
                    if k >= 1:
                        q = k - 1
                        dve.wait_ge(s["whi"], it * 3 + q + 1)
                        cols = bass.ds((it * 3 + q) * WC, WC)
                        V.tensor_tensor(wres[1][:, cols], wr[:, q, :], wres[0][:, cols].bitcast(F32),
                                        ALU.subtract).then_inc(s[f"wsp{q}"], 1)
                    dve.wait_ge(s[f"y{m}"], n + 1)
                    dve.wait_ge(s[f"yst{m}"], n * 16)
                    V.tensor_tensor(yo[:, m, :], yp[k], mk[:], ALU.mult).then_inc(s[f"ev{k}"], 1)

            evac(0)
            with dve.Fori(1, C // 4) as it:
                evac(it)
            dve.wait_ge(s["ev3"], C // 4)
            for q in range(3):
                dve.wait_ge(s[f"wsp{q}"], C // 4)
            dve.wait_ge(s["usp3"], C // 4)
            dve.wait_ge(s["tsp3"], C // 4)
            dve.sem_inc(s["done"], 1)
            dve.wait_ge(s["done"], 3)
            dve.sem_inc(s["accD"], 1)

            def x3_lo(i):
                for g in range(NG):
                    dve.wait_ge(s["x3hi"], i * NG + g + 1)
                    V.tensor_tensor(x3s[1][:, :, g * P:(g + 1) * P], x3p[g].rearrange("p (k n) -> p k n", k=KT),
                                    x3s[0][:, :, g * P:(g + 1) * P].bitcast(F32), ALU.subtract
                                    ).then_inc(s["x3lo"], 1)

            def t_mask(i):
                dve.wait_ge(s["la"], i + 1)
                for g in range(NG):
                    for u in range(2):
                        o = (2 * g + u) * P
                        last = V.tensor_tensor(
                            tsb[:, o:o + P].rearrange("p (q l r) -> p q l r", q=GB, l=2),
                            la[:, g * P:(g + 1) * P].rearrange("p (q u r) -> p q u r", q=GB, u=2)[:, :, u:u + 1, :]
                            .to_broadcast([P, GB, 2, RANK]),
                            blk.rearrange("p (q l r) -> p q l r", q=GB, l=2), ALU.mult)
                last.then_inc(s["tm"], 1)

            def t_low(i):
                dve.wait_ge(s["th"], i + 1)
                V.tensor_tensor(th[1][:].rearrange("p g u n -> p (g u n)"), la,
                                th[0][:].rearrange("p g u n -> p (g u n)").bitcast(F32), ALU.subtract
                                ).then_inc(s["tl"], 1)

            def act_mul(i, j):
                m = P if j < FT - 1 else FTAIL
                dve.wait_ge(s["silu"], i * FT + j + 1)
                V.tensor_tensor(sg[0:m, j % 2, :], sg[0:m, j % 2, :], wk[j % 2][0:m, TB:2 * TB], ALU.mult
                                ).then_inc(s["mul"], 1)

            x3_lo(0)
            t_mask(0)
            t_low(0)
            act_mul(0, 0)

            def dve_block(i, last):
                for j in range(1, FT):
                    act_mul(i, j)
                if not last:
                    x3_lo(i + 1)
                dve.wait_ge(s["tdone"], i + 1)
                V.tensor_tensor(tdm[:].rearrange("p (g q w) -> p g q w", g=NG, q=GB),
                                tdp[:, 0:NG * P].rearrange("p (g q w) -> p g q w", g=NG, q=GB),
                                blk.rearrange("p (q w) -> p q w", q=GB).unsqueeze(1).to_broadcast(
                                    [P, NG, GB, 2 * RANK]), ALU.mult).then_inc(s["tdm"], 1)
                dve.wait_ge(s["tdm"], i + 1)
                tq = tdm[:].rearrange("p (q l r) -> p q l r", l=2, r=RANK)
                V.tensor_tensor(tdd[:].rearrange("p g (q l r) -> p (g q) l r", l=2, r=RANK),
                                tq[:, :, 0:1, :].to_broadcast([P, NG * GB, 2, RANK]),
                                tq[:, :, 1:2, :].to_broadcast([P, NG * GB, 2, RANK]), ALU.add
                                ).then_inc(s["tdd"], 1)
                if not last:
                    t_mask(i + 1)
                    t_low(i + 1)
                dve.wait_ge(s["tdth"], i + 1)
                V.tensor_tensor(tdt[1][:].rearrange("p g n -> p (g n)"), tdp[:, 256:512],
                                tdt[0][:].rearrange("p g n -> p (g n)").bitcast(F32), ALU.subtract
                                ).then_inc(s["tdtl"], 1)
                if not last:
                    act_mul(i + 1, 0)
                dve.wait_ge(s["accd"], i + 1)
                V.tensor_copy(io[:, 1, :], acc[1]).then_inc(s["accD"], 1)

            with dve.Fori(0, NBLK - 1) as i:
                dve_block(i, False)
            dve_block(NBLK - 1, True)

        @block.tensor
        def _(pe):
            mm = nc.tensor.matmul
            pe.wait_ge(s["kst"], 1)
            for c in range(NCOND):
                last = mm(wmp[:, c * C:(c + 1) * C], w1s[:, c, :], w2s[:, c, :], start=True, stop=True)
            last.then_inc(s["wm"], 1)
            pe.wait_ge(s["kuv"], 1)
            for h in range(C):
                n, o = h // (C // 2), h % (C // 2) * UI
                last = mm(kp[n][:, o:o + UI], wtmp[:, 0, h * UN:(h + 1) * UN],
                          xs[:, X_V + h * UI:X_V + (h + 1) * UI], start=True, stop=True)
            last.then_inc(s["kps"], 1)
            PASSES = ((0, 0), (0, 1), (1, 0))

            def conv_block(it):
                for k in range(4):
                    m = k % 2
                    pe.wait_ge(s[f"usp{k}"], it + 1)
                    pe.wait_ge(s[f"tsp{k}"], it + 1)
                    pe.wait_ge(s[f"ev{k}"], it)
                    for c in range(KT):
                        for a, b in PASSES:
                            last = mm(yp[k][:, c * P:T], us[a][:, m, c * P:(c + 1) * P], ts_[b][:, m, 0:T - c * P],
                                      start=(c == 0 and a + b == 0), stop=(c == KT - 1 and a == 1))
                    last.then_inc(s[f"y{m}"], 1)

            conv_block(0)
            with pe.Fori(1, C // 4) as it:
                conv_block(it)
            pe.wait_ge(s["done"], 3)

            def mix_transposed(i):
                for g in range(NG):
                    for k in range(KT):
                        for a, b in PASSES:
                            last = mm(x3p[g][:, k * P:(k + 1) * P], x1s[a][:, g, k * P:(k + 1) * P],
                                      wbd[:, g, b, :], start=(a + b == 0), stop=(a == 1))
                    last.then_inc(s["x3mm"], 1)

            def lora_a(i):
                for g in range(NG):
                    for k in range(KT):
                        for a, b in PASSES:
                            w = ag[:, g * GB:(g + 1) * GB, b, :].rearrange("p q (u k r) -> p q u k r", u=2, k=KT)
                            last = mm(la[:, g * P:(g + 1) * P].rearrange("p (q u r) -> p q u r", q=GB, u=2),
                                      x3s[a][:, k, g * P:(g + 1) * P], w[:, :, :, k, :],
                                      start=(k == 0 and a + b == 0), stop=(k == KT - 1 and a == 1))
                last.then_inc(s["la"], 1)

            def lora_a_transposes(i):
                pe.wait_ge(s["tm"], i + 1)
                for q in range(2 * NG):
                    last = nc.tensor.transpose(la[:, q * P:(q + 1) * P], tsb[:, q * P:(q + 1) * P], ident)
                last.then_inc(s["tt"], 1)

            def gate_up(i, j):
                m = P if j < FT - 1 else FTAIL
                c = j // BJ
                for u in range(2):
                    o = wk[j % 2][0:m, u * TB:(u + 1) * TB]
                    for k in range(KT):
                        for a, b in PASSES:
                            mm(o, wgu[a][:, u, k, j * P:j * P + m], x3s[b][:, k, :],
                               start=(u == 0 and k == 0 and a + b == 0), stop=False, skip_group_check=True)
                    if j == 0 and u == 0:
                        lora_a_transposes(i)
                if j == 0:
                    pe.wait_ge(s["tl"], i + 1)
                if j % BJ == 0:
                    pe.wait_ge(s[f"b{c % 2}"], (i * (len(BCH) // 2) + c // 2 + 1) * 16 * BB)
                for u in range(2):
                    for g in range(NG):
                        for l in range(2):
                            last = mm(wk[j % 2][0:m, u * TB + g * P:u * TB + (g + 1) * P],
                                      bg[:, c % 2, g, j % BJ, u, 0:m], th[l][:, g, u, :],
                                      start=False, stop=(u == 1 and g == NG - 1 and l == 1), skip_group_check=True)
                last.then_inc(s["gu"], 1)

            def start_acc(i):
                for g in range(NG):
                    for n, (a, b) in enumerate(PASSES):
                        last = mm(acc[g], wbd[:, g, a, :], x1s[b][:, g, :], start=(n == 0), stop=False,
                                  skip_group_check=True)
                last.then_inc(s["accin"], 1)

            def down(i, j):
                m = P if j < FT - 1 else FTAIL
                adv = [adg[:, :, l, :].rearrange("p b (j r) -> p b j r", j=FT) for l in range(2)]
                for g in range(NG):
                    hi = ac[0][0:m, j % 2, g * P:(g + 1) * P]
                    lo = ac[1][0:m, j % 2, g * P:(g + 1) * P]
                    td3 = tdp[:, g * P:(g + 1) * P].rearrange("p (q l r) -> p q l r", q=GB, l=2)
                    adh = adg[0:m, g * GB:(g + 1) * GB, :, j * RANK:(j + 1) * RANK]
                    mm(acc[g], hi, wdn[0][0:m, j, :], start=False, stop=False, skip_group_check=True)
                    mm(acc[g], hi, wdn[1][0:m, j, :], start=False, stop=False, skip_group_check=True)
                    mm(td3, hi, adh, start=(j == 0 and g == 0), stop=False, skip_group_check=True)
                    mm(acc[g], lo, wdn[0][0:m, j, :], start=False, stop=False, skip_group_check=True)
                    last = mm(td3[:, :, 0, :], lo, adh[:, :, 0, :], start=False,
                              stop=(j == FT - 1 and g == NG - 1), skip_group_check=True)
                last.then_inc(s["tdone" if j == FT - 1 else "down"], 1)

            def lora_b_down(i):
                for g in range(NG):
                    for l in range(2):
                        last = mm(acc[g], tdt[l][:, g, :], bdg[:, g, :], start=False, stop=(l == 1),
                                  skip_group_check=True)
                last.then_inc(s["accd"], 1)

            def transposes(i):
                for g in range(NG):
                    last = nc.tensor.transpose(tdp[:, (NG + g) * P:(NG + g + 1) * P], tdd[:, g, :], ident)
                last.then_inc(s["tdx"], 1)

            def next_mix(i):
                pe.wait_ge(s["x1lo"], i * NG + NG)
                pe.wait_ge(s["wbd"], (i + 1) * 16 * BB)
                mix_transposed(i)

            next_mix(0)
            pe.wait_ge(s["x3lo"], NG)
            pe.wait_ge(s["ag"], 16 * BB)
            lora_a(0)
            gate_up(0, 0)

            def pe_block(i, last):
                for j in range(1, FT):
                    if j >= 2:
                        pe.wait_ge(s["mul"], i * FT + j - 1)
                    gate_up(i, j)
                    if j == 1:
                        pe.wait_ge(s["accA"], i + 1)
                        pe.wait_ge(s["accD"], i + 1)
                        start_acc(i)
                        pe.wait_ge(s["adg"], (i + 1) * 16 * BB)
                    pe.wait_ge(s["alo"], i * FT + j)
                    down(i, j - 1)
                    if j == 5 and not last:
                        next_mix(i + 1)
                pe.wait_ge(s["alo"], i * FT + FT)
                down(i, FT - 1)
                if not last:
                    pe.wait_ge(s["x3lo"], i * NG + 2 * NG)
                    pe.wait_ge(s["ag"], (i + 2) * 16 * BB)
                    lora_a(i + 1)
                pe.wait_ge(s["tdd"], i + 1)
                transposes(i)
                if not last:
                    pe.wait_ge(s["mul"], i * FT + FT)
                    gate_up(i + 1, 0)
                pe.wait_ge(s["tdtl"], i + 1)
                pe.wait_ge(s["bdg"], (i + 1) * 16 * BB)
                lora_b_down(i)

            with pe.Fori(0, NBLK - 1) as i:
                pe_block(i, False)
            pe_block(NBLK - 1, True)


def kernel(**inputs):
    import numpy as np
    import concourse.bacc as bacc
    from concourse import mybir as mb
    from concourse.bass_utils import run_bass_kernel_spmd

    g = {k: np.ascontiguousarray(v) for k, v in inputs.items()}
    x = g["x"]
    xT = x.transpose(1, 2, 0).reshape(C, KT, P, B)[:, :, ::-1].transpose(0, 2, 1, 3).reshape(C, P, KT * B)

    def twice(a):
        return np.concatenate([a.T, a.T], axis=0)

    ssm = np.stack([twice(g["L0_cond_log_A_real"]), twice(g["L0_cond_A_imag"]), twice(g["L0_cond_C"][..., 0]),
                    twice(g["L0_cond_C"][..., 1]), np.broadcast_to(g["L0_cond_log_dt"], (P, C))], axis=1)
    cst = np.zeros((P, K_N), np.float32)
    cst[:, K_ID:K_ID + P] = np.eye(P)
    cst[:, K_BLK:K_BLK + P] = 0.5 * np.kron(np.eye(GB), np.ones((C, C)))
    cst[:, K_T:K_T + T] = np.arange(T)
    cst[:, K_PU:K_PU + UN] = UI * np.arange(UN)
    cst[:, K_PV:K_PV + UI] = np.arange(UI)
    cst[:NS, K_S] = 1.0
    cst[NS:, K_S + 1] = 1.0
    cst[:NS, K_S + 2] = 0.25
    cst[:NS, K_S + 3] = np.pi / 2

    def hidden(w):
        o = np.zeros((P, KT, FP), np.float32)
        o[:, :, :F] = w.T.reshape(KT, P, F).transpose(1, 0, 2)
        return o.reshape(P, KT * FP)

    wd = np.zeros((FP, T), np.float32)
    wd[:F] = g["L3_cond_W_down"].T
    wall = np.concatenate([hidden(g["L3_cond_W_gate"]), hidden(g["L3_cond_W_up"]),
                           wd.reshape(FT, P, T).transpose(1, 0, 2).reshape(P, FT * T)], axis=1)
    a2 = np.stack([g["L3_cond_A_gate"][0], g["L3_cond_A_up"][0]], axis=1)
    ta = a2.reshape(NA, 2, RANK, KT, P).transpose(4, 0, 1, 3, 2).reshape(P, NA, WA)
    ad = np.zeros((NA, RANK, FP), np.float32)
    ad[:, :, :F] = g["L3_cond_A_down"][0]
    tad = ad.reshape(NA, RANK, FT, P).transpose(3, 0, 2, 1).reshape(P, NA, WAD)
    b2 = np.zeros((NA, RANK, 2, FP), np.float32)
    b2[:, :, 0, :F] = g["L3_cond_B_gate"][0].transpose(0, 2, 1)
    b2[:, :, 1, :F] = g["L3_cond_B_up"][0].transpose(0, 2, 1)
    tb = b2.reshape(NA, RANK, 2, FT, P).transpose(0, 1, 3, 2, 4).reshape(2, P, WB)
    tbd = g["L3_cond_B_down"][0].transpose(0, 2, 1).reshape(2, P, WBD).transpose(1, 0, 2)

    arrays = {
        "xT": xT, "x": x.reshape(B * C, T), "lens": g["itok_B_78_3631"].reshape(B, 1),
        "cidx": g["itok_B_0_15"].reshape(1, B), "lidx": g["itok_B_2_6"].reshape(1, B), "ssm": ssm,
        "dskip": g["L0_cond_D"].reshape(1, C), "cst": cst, "w1t": g["L1_cond_weights"].transpose(2, 0, 1),
        "w2": g["L2_cond_weights"].transpose(1, 0, 2), "wall": wall, "ta": ta, "tad": tad, "tb": tb, "tbd": tbd,
    }
    nc = bacc.Bacc("TRN2", target_bir_lowering=False, num_devices=1)
    feeds, args = {}, []
    for name, a in arrays.items():
        a = np.ascontiguousarray(a)
        feeds["in_" + name] = a
        args.append(nc.dram_tensor("in_" + name, a.shape, mb.dt.from_np(a.dtype), kind="ExternalInput").ap())
    args.append(nc.dram_tensor("out_x", (B * C, T), mb.dt.from_np(np.dtype("float32")), kind="ExternalOutput").ap())
    cond_resid_kernel(nc, *args)
    r = run_bass_kernel_spmd(nc, [feeds], core_ids=[0])
    return r.results[0]["out_x"].reshape(B, C, T)
```

```python
import math
from contextlib import ExitStack

import concourse.bass as bass
from concourse import mybir

ALU = mybir.AluOpType
ACT = mybir.ActivationFunctionType
F32 = mybir.dt.float32
F32R = mybir.dt.float32r
I32 = mybir.dt.int32

B, C, T = 128, 32, 512
NS = 64
NCOND = 16
F = 1376
NA, RANK = 16, 16
P = 128
KT = T // P
FT = -(-F // P)
FTAIL = F - (FT - 1) * P
FP = FT * P
UI, UN = 32, T // 32
GB = P // C
NG = 2
BB = NG * GB
TB = BB * C
NBLK = B // BB
WC = 704
WGU = 2 * KT * FP
WCOLS = WGU + FT * T
NWC = WCOLS // WC
BJ = 2
BCH = [list(range(j, min(j + BJ, FT))) for j in range(0, FT, BJ)]
WA, WAD, WB, WBD = 2 * KT * RANK, FT * RANK, FT * 2 * P, T
XJ = (4, 7)
WBDJ = {2: (0, 1, 2), 3: (3, 4, 5), 4: (6, 7)}
AGJ = {5: (0, 1, 2), 6: (3, 4, 5), 8: (6, 7)}
MIXJ = 9
ROUND = 12582912.0
PIC = 3.1415925
C1 = 6.28125
C2 = 2.0 * math.pi - C1
K_ID, K_BLK, K_T, K_PU, K_PV, K_S = 0, 128, 256, 768, 784, 816
K_N = 824
UCOLS, VCOLS = C * UN, C * UI
X_SB = UCOLS
X_SBH = UCOLS + C
X_COS = UCOLS + 2 * C
X_CB = X_COS + UCOLS
X_V = X_CB + C
X_N = X_V + VCOLS


def cond_resid_kernel(nc, xT, x, lens, cidx, lidx, ssm, dskip, cst, w1t, w2, wall, ta, tad, tb, tbd, out):
    kpad = nc.dram_tensor("kpad", (C, P + T), F32, kind="Internal").ap()
    x1p = nc.dram_tensor("x1p", (B * C, T), F32, kind="Internal").ap()
    tm_d = nc.dram_tensor("tm_d", (NCOND, C, 2, C), F32, kind="Internal").ap()
    ta_d = nc.dram_tensor("ta_d", (NA, P, 2, WA), F32, kind="Internal").ap()
    tad_d = nc.dram_tensor("tad_d", (NA, P, 2, WAD), F32, kind="Internal").ap()
    tb_d = nc.dram_tensor("tb_d", (NA, 2 * RANK, WB), F32, kind="Internal").ap()
    tbd_d = nc.dram_tensor("tbd_d", (NA, 2 * RANK, WBD), F32, kind="Internal").ap()
    x1p_bct = x1p.rearrange("(b c) t -> b c t", c=C)

    ctx = ExitStack()
    with ctx:
        def sem(name):
            return ctx.enter_context(nc.semaphore(name))

        def sbin(stack):
            return lambda name, shape, dt=F32: stack.enter_context(nc.sbuf_tensor(name, shape, dt))

        ps = ctx.enter_context(nc.psum_tensor("ps", [P, 8, 512], F32))
        acc = [ps[:, g, :] for g in range(NG)]
        x3p = [ps[:, 2 + g, :] for g in range(NG)]
        wk = [ps[:, 4 + n, :] for n in range(2)]
        la = ps[:, 6, :]
        tdp = ps[:, 7, :]
        yp = [ps[:, n, :] for n in range(4)]
        kp = [ps[0:UN, 6 + n, :] for n in range(2)]
        wmp = ps[0:C, 5, :]

        sb = sbin(ctx)
        cs = sb("cs", [P, K_N])
        ixs = sb("ixs", [1, 2 * B], I32)
        prep = ExitStack()
        sb = sbin(prep)
        pk = sb("pk", [P, 5, C])
        dsk = sb("dsk", [1, C])
        xs = sb("xs", [P, X_N])
        kk = sb("kk", [P, X_N])
        ex = sb("ex", [P, UCOLS + VCOLS])
        sm = sb("sm", [P, 24, C])
        zer = sb("zer", [C, P])
        kf = sb("kf", [UN, C, UI])
        w1s = sb("w1s", [C, NCOND, C])
        w2s = sb("w2s", [C, NCOND, C])
        wms = sb("wms", [C, NCOND, 2, C])
        ta_r = sb("ta_r", [P, NA, WA])
        tad_r = sb("tad_r", [P, NA, WAD])
        tb_r = sb("tb_r", [P, 2, WB])
        tbd_r = sb("tbd_r", [P, 2, WBD])
        ta_h = sb("ta_h", [P, NA, WA])
        tad_h = sb("tad_h", [P, NA, WAD])
        tb_h = sb("tb_h", [P, 2, WB])
        tbd_h = sb("tbd_h", [P, 2, WBD])
        prep.close()
        sb = sbin(ctx)
        wres = [sb("w_hi", [P, WCOLS], F32R), sb("w_lo", [P, WCOLS], F32R)]
        conv = ExitStack()
        sb = sbin(conv)
        ur = sb("ur", [P, 4, KT * B])
        tr = sb("tr", [P, 4, T])
        us = [sb("us_hi", [P, 4, KT * B], F32R), sb("us_lo", [P, 4, KT * B], F32R)]
        ts_ = [sb("ts_hi", [P, 4, T], F32R), sb("ts_lo", [P, 4, T], F32R)]
        yo = sb("yo", [P, 4, T])
        wr = sb("wr", [P, 3, WC])
        mk = sb("mk", [P, T])
        leni = sb("leni", [P, 1], I32)
        lenf = sb("lenf", [P, 1])
        conv.close()
        sb = sbin(ctx)
        ag = sb("ag", [P, BB, 2, WA], F32R)
        adg = sb("adg", [P, BB, 2, WAD], F32R)
        bg = sb("bg", [P, 2, NG, BJ, 2, P], F32R)
        bdg = sb("bdg", [P, NG, WBD], F32R)
        x1s = [sb("x1_hi", [P, NG, T], F32R), sb("x1_lo", [P, NG, T], F32R)]
        io = sb("io", [P, 2, T])
        wbd = sb("wbd", [P, NG, 2, P], F32R)
        x3s = [sb("x3_hi", [P, KT, TB], F32R), sb("x3_lo", [P, KT, TB], F32R)]
        tsb = sb("tsb", [P, NG * 2 * P])
        th = [sb("t_hi", [P, NG, 2, P], F32R), sb("t_lo", [P, NG, 2, P], F32R)]
        sg = sb("sg", [P, 2, TB])
        ac = [sb("act_hi", [P, 2, TB], F32R), sb("act_lo", [P, 2, TB], F32R)]
        tdm = sb("tdm", [P, NG * P])
        tdd = sb("tdd", [P, NG, P])
        tdt = [sb("tdt_hi", [P, NG, P], F32R), sb("tdt_lo", [P, NG, P], F32R)]

        names = """pk cst small lens tabs w12 zer kf kst kout wm wms tst u0 u1 tt0 tt1 wl0 wl1 wl2
            a1 dch ph ex tg tab0 tab1 tab2 tab3 kuv kps uhi thi usp0 usp1 usp2 usp3 tsp0 tsp1 tsp2 tsp3 whi wsp0 wsp1 wsp2 y0 y1 y2 y3
            ev0 ev1 ev2 ev3 yst0 yst1 mask done tah tal tbh tbl tbs prepped
            tt ag adg b0 b1 bdg wbd xin xsum x1hi x1lo x3mm x3hi x3lo la tm th tl gu silu mul ahi alo down accin
            tdone tdm tdd tdx tdth tdtl accd accA accD ost wz""".split()
        s = {n: sem("s_" + n) for n in names}

        def at(eng, value):
            return value if isinstance(value, int) else eng.snap(value)

        wgu = [w[:, 0:WGU].rearrange("p (u k f) -> p u k f", u=2, k=KT) for w in wres]
        wdn = [w[:, WGU:WCOLS].rearrange("p (j t) -> p j t", j=FT) for w in wres]
        ident = cs[:, K_ID:K_ID + P]
        blk = cs[:, K_BLK:K_BLK + P]
        tvals = cs[:, K_T:K_T + T]

        NST = 9

        def load_toeplitz(eng, h, p):
            src = kpad[bass.ds(h, 2), 0:T] if not isinstance(h, int) else kpad[h:h + 2, 0:T]
            src = bass.AP(src.tensor, src.offset, [[1, P], [P + T, 2], [1, T]])
            eng.dma_start(tr[:, 2 * p:2 * p + 2, :], src).then_inc(s[f"tt{p}"], 16)

        def rows_of(b):
            return b // GB, (b % GB) * C, (b % GB + 1) * C

        def entry(eng, column, count):
            return bass.ds(eng.value_load(ixs[0:1, bass.ds(column, 1)], min_val=0, max_val=count - 1), 1)

        block = ctx.enter_context(nc.Block())

        @block.sync
        def _(sp):
            sp.dma_start(pk[:], ssm).then_inc(s["pk"], 16)
            sp.dma_start(cs[:], cst).then_inc(s["cst"], 16)
            sp.dma_start(w1s[:], w1t).then_inc(s["w12"], 16)
            sp.dma_start(w2s[:], w2).then_inc(s["w12"], 16)
            sp.dma_start(dsk[:], dskip).then_inc(s["small"], 16)
            sp.dma_start(leni[:], lens).then_inc(s["lens"], 16)
            sp.dma_start(ixs[:, 0:B], lidx).then_inc(s["small"], 16)
            sp.dma_start(ixs[:, B:2 * B], cidx).then_inc(s["small"], 16)
            for p in range(2):
                sp.dma_start(ur[:, 2 * p:2 * p + 2, :], xT[2 * p:2 * p + 2].rearrange("c p w -> p c w")
                             ).then_inc(s[f"u{p}"], 16)
            for n, (dst, src) in enumerate(((tb_r, tb), (ta_r, ta), (tad_r, tad), (tbd_r, tbd))):
                sp.dma_start(dst[:], src).then_inc(s[f"tab{n}"], 16)
            for q in range(3):
                sp.dma_start(wr[:, q, :], wall[:, q * WC:(q + 1) * WC]).then_inc(s[f"wl{q}"], 16)
            sp.wait_ge(s["wms"], 2)
            sp.dma_start(tm_d.rearrange("s c l d -> c s l d"), wms[:]).then_inc(s["tst"], 16)
            tables = ((tb_d.rearrange("(n a) (r l) w -> (a r) n l w", n=2, l=2), tb_h, tb_r),
                      (ta_d.rearrange("a p l w -> p a l w"), ta_h, ta_r),
                      (tad_d.rearrange("a p l w -> p a l w"), tad_h, tad_r),
                      (tbd_d.rearrange("(n a) (r l) w -> (a r) n l w", n=2, l=2), tbd_h, tbd_r))
            for n, (dst, hi, lo) in enumerate(tables):
                for half, src, g in ((0, hi, "tah"), (1, lo, "tal")):
                    sp.wait_ge(s[g], n + 1)
                    sp.dma_start(dst[:, :, half, :], src[:]).then_inc(s["tst"], 16)

            def conv_io(it, last):
                nxt = [at(sp, it * 4 + 4 + 2 * p) for p in range(2)]
                here = [at(sp, it * 4 + 2 * p) for p in range(2)]
                chunk = [at(sp, (it * 3 + q + 3) * WC) for q in range(3)]
                for p in range(2):
                    if not last:
                        sp.wait_ge(s[f"usp{2 * p}"], it + 1)
                        sp.wait_ge(s[f"usp{2 * p + 1}"], it + 1)
                        sp.dma_start(ur[:, 2 * p:2 * p + 2, :],
                                     xT[bass.ds(nxt[p], 2)].rearrange("c p w -> p c w")).then_inc(s[f"u{p}"], 16)
                        sp.wait_ge(s[f"tsp{2 * p}"], it + 1)
                        sp.wait_ge(s[f"tsp{2 * p + 1}"], it + 1)
                        load_toeplitz(sp, nxt[p], p)
                        for q in ((0,), (1, 2))[p]:
                            sp.wait_ge(s[f"wsp{q}"], it + 1)
                            sp.dma_start(wr[:, q, :], wall[:, bass.ds(chunk[q], WC)]).then_inc(s[f"wl{q}"], 16)
                    sp.wait_ge(s[f"ev{2 * p}"], it + 1)
                    sp.wait_ge(s[f"ev{2 * p + 1}"], it + 1)
                    sp.dma_start(x1p_bct[:, bass.ds(here[p], 2), :], yo[:, 2 * p:2 * p + 2, :]
                                 ).then_inc(s[f"yst{p}"], 16)

            with sp.Fori(0, C // 4 - 1) as it:
                conv_io(it, False)
            conv_io(C // 4 - 1, True)
            sp.wait_ge(s["tst"], 16 * NST)
            sp.wait_ge(s["yst0"], 16 * C // 4)
            sp.wait_ge(s["yst1"], 16 * C // 4)
            sp.wait_ge(s["done"], 3)
            sp.wait_ge(s["wz"], 1)

            def entries(i):
                return [entry(sp, i * BB + b, NA) for b in range(BB)]

            def load_adg(e, free):
                if free is not None:
                    sp.wait_ge(*free)
                for b in range(BB):
                    sp.dma_start(adg[:, b, :, :].bitcast(F32), tad_d[e[b]].rearrange("a p l w -> (a p) l w")
                                 ).then_inc(s["adg"], 16)

            def load_b(e, c, free):
                if free is not None:
                    sp.wait_ge(*free)
                o, w = BCH[c][0] * 2 * P, len(BCH[c]) * 2 * P
                for b in range(BB):
                    g, p0, p1 = rows_of(b)
                    sp.dma_start(bg[p0:p1, c % 2, g, :, :, :].rearrange("p j u f -> p (j u f)")[:, 0:w].bitcast(F32),
                                 tb_d[e[b], :, o:o + w].rearrange("a k w -> (a k) w")).then_inc(s[f"b{c % 2}"], 16)

            def load_bdg(e, free):
                if free is not None:
                    sp.wait_ge(*free)
                for b in range(BB):
                    g, p0, p1 = rows_of(b)
                    sp.dma_start(bdg[p0:p1, g, :].bitcast(F32), tbd_d[e[b]].rearrange("a k w -> (a k) w")
                                 ).then_inc(s["bdg"], 16)

            def load_x(i, g, stored=None):
                first = at(sp, i * TB + g * P)
                if stored is not None:
                    sp.wait_ge(s["ost"], stored)
                if g > 0:
                    sp.wait_ge(s["x1lo"], i * NG + g)
                sp.dma_start(io[:, 0, :], x1p[bass.ds(first, P), :]).then_inc(s["xin"], 16)
                sp.dma_start(io[:, 1, :], x[bass.ds(first, P), :]).then_inc(s["xin"], 16)

            e0 = entries(0)
            sp.sem_inc(s["ost"], 16)
            load_x(0, 0)
            load_b(e0, 0, None)
            load_x(0, 1)
            load_b(e0, 1, None)
            load_adg(e0, None)
            load_bdg(e0, None)

            def block_io(i, last):
                here = entries(i)
                for c in range(2, len(BCH) + 2):
                    free = (s["gu"], i * FT + BCH[c - 2][-1] + 1)
                    if c < len(BCH):
                        load_b(here, c, free)
                    elif not last:
                        load_b(ahead, c - len(BCH), free)
                    if c == 2 and not last:
                        load_x(i + 1, 0, i * 16 * NG + 16)
                    if c == 3 and not last:
                        ahead = entries(i + 1)
                    if c == 4 and not last:
                        load_x(i + 1, 1)
                if not last:
                    load_adg(ahead, (s["tdone"], i + 1))
                    load_bdg(ahead, (s["accd"], i + 1))
                first = [at(sp, i * TB + g * P) for g in range(NG)]
                for g, name in enumerate(("accA", "accD")):
                    sp.wait_ge(s[name], i + 2)
                    sp.dma_start(out[bass.ds(first[g], P), :], io[:, g, :]).then_inc(s["ost"], 16)

            with sp.Fori(0, NBLK - 1) as i:
                block_io(i, False)
            block_io(NBLK - 1, True)
            sp.wait_ge(s["ost"], 16 * NG * NBLK + 16)

        @block.gpsimd
        def _(pool):
            nc.gpsimd.memset(zer[:], 0.0).then_inc(s["zer"], 1)
            for n, (hi, raw) in enumerate(((tb_h, tb_r), (ta_h, ta_r), (tad_h, tad_r), (tbd_h, tbd_r))):
                pool.wait_ge(s["tah"], n + 1)
                nc.gpsimd.tensor_tensor(raw[:].bitcast(F32R), raw[:], hi[:], ALU.subtract).then_inc(s["tal"], 1)

            def lows(it):
                for k in range(4):
                    if k % 2 == 0:
                        pool.wait_ge(s["uhi"], it * 4 + k + 1)
                        nc.gpsimd.tensor_tensor(us[1][:, k, :], ur[:, k, :], us[0][:, k, :].bitcast(F32),
                                                ALU.subtract).then_inc(s[f"usp{k}"], 1)
                    pool.wait_ge(s["thi"], it * 4 + k + 1)
                    nc.gpsimd.tensor_tensor(ts_[1][:, k, :], tr[:, k, :], ts_[0][:, k, :].bitcast(F32),
                                            ALU.subtract).then_inc(s[f"tsp{k}"], 1)

            with pool.Fori(0, C // 4) as it:
                lows(it)
            pool.wait_ge(s["done"], 2)
            pool.wait_ge(s["yst0"], 16 * C // 4)
            pool.wait_ge(s["yst1"], 16 * C // 4)
            nc.gpsimd.memset(wbd[:].bitcast(F32), 0.0).then_inc(s["wz"], 1)
            pool.wait_ge(s["wz"], 1)
            pool.sem_inc(s["done"], 1)

            def block_sum(i, g):
                if True:
                    pool.wait_ge(s["xin"], (i * NG + g + 1) * 32)
                    nc.gpsimd.tensor_tensor(io[:, 0, :], io[:, 0, :], io[:, 1, :], ALU.add).then_inc(s["xsum"], 1)
                    pool.wait_ge(s["x1hi"], i * NG + g + 1)
                    nc.gpsimd.tensor_tensor(x1s[1][:, g, :], io[:, 0, :], x1s[0][:, g, :].bitcast(F32),
                                            ALU.subtract).then_inc(s["x1lo"], 1)

            block_sum(0, 0)
            block_sum(0, 1)

            def lows3(i, last):
                for j in range(FT):
                    m = P if j < FT - 1 else FTAIL
                    pool.wait_ge(s["ahi"], i * FT + j + 1)
                    nc.gpsimd.tensor_tensor(ac[1][0:m, j % 2, :], sg[0:m, j % 2, :], ac[0][0:m, j % 2, :].bitcast(F32),
                                            ALU.subtract).then_inc(s["alo"], 1)
                    if j in XJ and not last:
                        block_sum(i + 1, XJ.index(j))

            with pool.Fori(0, NBLK - 1) as i:
                lows3(i, False)
            lows3(NBLK - 1, True)

        @block.scalar
        def _(act):
            act.wait_ge(s["pk"], 16)
            nc.scalar.activation(sm[:, 0, :], pk[:, 4, :], ACT.Exp).then_inc(s["a1"], 1)
            nc.scalar.activation(sm[:, 1, :], pk[:, 0, :], ACT.Exp).then_inc(s["a1"], 1)
            act.wait_ge(s["ex"], 1)
            nc.scalar.activation(sm[:, 4, :], sm[:, 2, :], ACT.Tanh, scale=0.5).then_inc(s["a1"], 1)
            nc.scalar.activation(ex[:], ex[:], ACT.Exp).then_inc(s["a1"], 1)
            act.wait_ge(s["ph"], 1)
            for lo, hi, off in ((0, X_COS, None), (X_COS, X_V, K_S + 4), (X_V, X_N, K_S + 3)):
                last = nc.scalar.activation(xs[:, lo:hi], xs[:, lo:hi], ACT.Sin,
                                            **({} if off is None else {"bias": cs[:, off:off + 1]}))
            last.then_inc(s["tg"], 1)
            act.wait_ge(s["wm"], 1)
            wm3 = wmp.rearrange("c (s d) -> c s d", d=C)
            nc.scalar.activation(wms[:, :, 0, :].bitcast(F32R), wm3, ACT.Copy).then_inc(s["wms"], 1)
            for n, (hi, raw) in enumerate(((tb_h, tb_r), (ta_h, ta_r), (tad_h, tad_r), (tbd_h, tbd_r))):
                act.wait_ge(s[f"tab{n}"], 16)
                nc.scalar.activation(hi[:].bitcast(F32R), raw[:], ACT.Copy).then_inc(s["tah"], 1)
            act.wait_ge(s["zer"], 1)
            act.dma_start(kpad[:, 0:P - 1], zer[:, 0:P - 1]).then_inc(s["kout"], 16)
            act.wait_ge(s["kf"], 1)
            act.dma_start(kpad[:, P - 1:P - 1 + T].rearrange("h (i j) -> i h j", j=UI), kf[:]).then_inc(s["kout"], 16)
            act.wait_ge(s["kout"], 32)
            for p in range(2):
                load_toeplitz(act, 2 * p, p)

            def highs(it, first):
                for k in range(4):
                    act.wait_ge(s[f"u{k // 2}"], it * 16 + 16)
                    if not first:
                        act.wait_ge(s[f"y{k}"], it)
                    nc.scalar.activation(us[0][:, k, :], ur[:, k, :], ACT.Copy).then_inc(s["uhi"], 1)
                    act.wait_ge(s[f"tt{k // 2}"], it * 16 + 16)
                    nc.scalar.activation(ts_[0][:, k, :], tr[:, k, :], ACT.Copy).then_inc(s["thi"], 1)
                    if first and k == 1:
                        act.wait_ge(s["tst"], 16 * NST)
                    if k >= 1:
                        q = k - 1
                        act.wait_ge(s[f"wl{q}"], it * 16 + 16)
                        nc.scalar.activation(wres[0][:, bass.ds((it * 3 + q) * WC, WC)], wr[:, q, :],
                                             ACT.Copy).then_inc(s["whi"], 1)

            highs(0, True)
            with act.Fori(1, C // 4) as it:
                highs(it, False)
            for k in range(4):
                act.wait_ge(s[f"y{k}"], C // 4)
            act.sem_inc(s["done"], 1)
            act.wait_ge(s["done"], 3)
            act.sem_inc(s["accA"], 1)

            def x1_hi(i, groups):
                for g in groups:
                    act.wait_ge(s["xsum"], i * NG + g + 1)
                    nc.scalar.activation(x1s[0][:, g, :], io[:, 0, :], ACT.Copy).then_inc(s["x1hi"], 1)

            def load_ag(i, batches):
                for b in batches:
                    e = entry(act, i * BB + b, NA)
                    act.dma_start(ag[:, b, :, :].bitcast(F32), ta_d[e].rearrange("a p l w -> (a p) l w")
                                  ).then_inc(s["ag"], 16)

            def load_wbd(i, batches):
                for b in batches:
                    g, p0, p1 = rows_of(b)
                    e = entry(act, i * BB + b + B, NCOND)
                    act.dma_start(wbd[p0:p1, g, :, p0:p1].bitcast(F32), tm_d[e].rearrange("a c l d -> (a c) l d")
                                  ).then_inc(s["wbd"], 16)

            def x3_hi(i):
                for g in range(NG):
                    act.wait_ge(s["x3mm"], i * NG + g + 1)
                    nc.scalar.activation(x3s[0][:, :, g * P:(g + 1) * P],
                                         x3p[g].rearrange("p (k n) -> p k n", k=KT), ACT.Copy).then_inc(s["x3hi"], 1)

            def t_hi(i):
                act.wait_ge(s["tt"], i + 1)
                nc.scalar.activation(th[0][:].rearrange("p g u n -> p (g u n)"), la, ACT.Copy
                                     ).then_inc(s["th"], 1)

            def act_tile(i, j):
                m = P if j < FT - 1 else FTAIL
                act.wait_ge(s["gu"], i * FT + j + 1)
                nc.scalar.activation(sg[0:m, j % 2, :], wk[j % 2][0:m, 0:TB], ACT.Silu).then_inc(s["silu"], 1)
                act.wait_ge(s["mul"], i * FT + j + 1)
                nc.scalar.activation(ac[0][0:m, j % 2, :], sg[0:m, j % 2, :], ACT.Copy).then_inc(s["ahi"], 1)

            load_wbd(0, range(BB))
            x1_hi(0, range(NG))
            load_ag(0, range(BB))
            x3_hi(0)
            t_hi(0)
            act_tile(0, 0)

            def act_block(i, last):
                for j in range(1, FT):
                    act_tile(i, j)
                    if last:
                        continue
                    if j == 2:
                        act.wait_ge(s["accin"], i + 1)
                    if j in WBDJ:
                        load_wbd(i + 1, WBDJ[j])
                    if j in AGJ:
                        load_ag(i + 1, AGJ[j])
                    if j in XJ:
                        x1_hi(i + 1, (XJ.index(j),))
                if not last:
                    x3_hi(i + 1)
                    t_hi(i + 1)
                act.wait_ge(s["tdx"], i + 1)
                nc.scalar.activation(tdt[0][:].rearrange("p g n -> p (g n)"), tdp[:, 256:512], ACT.Copy
                                     ).then_inc(s["tdth"], 1)
                if not last:
                    act_tile(i + 1, 0)
                act.wait_ge(s["accd"], i + 1)
                nc.scalar.activation(io[:, 0, :], acc[0], ACT.Copy).then_inc(s["accA"], 1)

            with act.Fori(0, NBLK - 1) as i:
                act_block(i, False)
            act_block(NBLK - 1, True)

        @block.vector
        def _(dve):
            chain = [0]

            def link(ins):
                chain[0] += 1
                ins.then_inc(s["dch"], 1)
                dve.wait_ge(s["dch"], chain[0])

            V = nc.vector
            dve.wait_ge(s["a1"], 2)
            dve.wait_ge(s["cst"], 16)

            def v(n):
                return sm[:, n, :]

            DT, EA, A_, BI, TH = 0, 1, 2, 3, 4
            aim, cr, ci = pk[:, 1, :], pk[:, 2, :], pk[:, 3, :]
            link(V.scalar_tensor_tensor(out=v(A_), in0=v(EA), scalar=-1.0, in1=v(DT), op0=ALU.mult, op1=ALU.mult))
            link(V.tensor_tensor(v(BI), aim, v(DT), ALU.mult))
            pu = cs[:, K_PU:K_PU + UN]
            pv = cs[:, K_PV:K_PV + UI]

            def outer(dst, col, powers, n):
                return V.tensor_tensor(dst.rearrange("p (h n) -> p h n", n=n),
                                       v(col).unsqueeze(2).to_broadcast([P, C, n]),
                                       powers.unsqueeze(1).to_broadcast([P, C, n]), ALU.mult)

            outer(ex[:, 0:UCOLS], A_, pu, UN)
            outer(ex[:, UCOLS:], A_, pv, UI).then_inc(s["ex"], 1)
            outer(xs[:, 0:UCOLS], BI, pu, UN)
            outer(xs[:, X_COS:X_COS + UCOLS], BI, pu, UN)
            outer(xs[:, X_V:X_N], BI, pv, UI)
            V.tensor_copy(xs[:, X_SB:X_SB + C], v(BI))
            V.tensor_copy(xs[:, X_CB:X_CB + C], v(BI))
            link(V.tensor_scalar(xs[:, X_SBH:X_SBH + C], v(BI), 0.5, None, ALU.mult))
            i2p = 1.0 / (2.0 * math.pi)
            col = [cs[:, K_S + n:K_S + n + 1] for n in range(8)]
            parts = ((0, X_COS, 0.0, PIC, -PIC), (X_COS, X_V, 0.25, PIC - math.pi / 2, -PIC - math.pi / 2),
                     (X_V, X_N, col[2], col[5], col[6]))
            for lo, hi, turn, _, _ in parts:
                last = V.tensor_scalar(kk[:, lo:hi], xs[:, lo:hi], i2p, turn, ALU.mult, ALU.add)
            link(last)
            link(V.tensor_scalar(kk[:], kk[:], ROUND, -ROUND, ALU.add, ALU.add))
            for c in (C1, C2):
                link(V.scalar_tensor_tensor(out=xs[:], in0=kk[:], scalar=-c, in1=xs[:], op0=ALU.mult, op1=ALU.add))
            for lo, hi, _, top, bottom in parts:
                last = V.tensor_scalar(xs[:, lo:hi], xs[:, lo:hi], top, bottom, ALU.min, ALU.max)
            last.then_inc(s["ph"], 1)
            dve.wait_ge(s["w12"], 32)
            idc = cs[0:C, K_ID:K_ID + C].unsqueeze(1).to_broadcast([C, NCOND, C])
            V.tensor_tensor(w1s[:], w1s[:], idc, ALU.add)
            V.tensor_tensor(w2s[:], w2s[:], idc, ALU.add).then_inc(s["kst"], 1)
            dve.wait_ge(s["a1"], 4)
            OM, RC, EM, A2, I2, ER, EI, GR, GI, TR_, TI = 5, 6, 7, 8, 9, 10, 11, 12, 13, 14, 15
            T1, T2, PP, QQ = 16, 17, 18, 19
            link(V.tensor_scalar(v(OM), v(TH), -1.0, 1.0, ALU.mult, ALU.add))
            link(V.reciprocal(v(RC), v(OM)))
            link(V.scalar_tensor_tensor(out=v(EM), in0=v(TH), scalar=2.0, in1=v(RC), op0=ALU.mult, op1=ALU.mult))
            link(V.tensor_tensor(v(A2), v(EA), v(EA), ALU.mult))
            link(V.tensor_tensor(v(T1), aim, aim, ALU.mult))
            link(V.tensor_tensor(v(A2), v(A2), v(T1), ALU.add))
            link(V.reciprocal(v(I2), v(A2)))
            dve.wait_ge(s["tg"], 1)
            sb_, cb, sbh = xs[:, X_SB:X_SB + C], xs[:, X_CB:X_CB + C], xs[:, X_SBH:X_SBH + C]
            link(V.tensor_tensor(v(T1), sbh, sbh, ALU.mult))
            link(V.tensor_tensor(v(ER), v(EM), cb, ALU.mult))
            link(V.scalar_tensor_tensor(out=v(ER), in0=v(T1), scalar=-2.0, in1=v(ER), op0=ALU.mult, op1=ALU.add))
            link(V.scalar_tensor_tensor(out=v(EI), in0=v(EM), scalar=1.0, in1=sb_, op0=ALU.add, op1=ALU.mult))
            link(V.tensor_tensor(v(T1), v(EI), aim, ALU.mult))
            link(V.tensor_tensor(v(T2), v(ER), v(EA), ALU.mult))
            link(V.tensor_tensor(v(T1), v(T1), v(T2), ALU.subtract))
            link(V.tensor_tensor(v(GR), v(T1), v(I2), ALU.mult))
            link(V.tensor_tensor(v(T1), v(EI), v(EA), ALU.mult))
            link(V.tensor_tensor(v(T2), v(ER), aim, ALU.mult))
            link(V.tensor_tensor(v(T1), v(T1), v(T2), ALU.add))
            link(V.scalar_tensor_tensor(out=v(GI), in0=v(T1), scalar=-1.0, in1=v(I2), op0=ALU.mult, op1=ALU.mult))
            link(V.tensor_tensor(v(T1), cr, v(GR), ALU.mult))
            link(V.tensor_tensor(v(T2), ci, v(GI), ALU.mult))
            link(V.tensor_tensor(v(TR_), v(T1), v(T2), ALU.subtract))
            link(V.tensor_tensor(v(T1), cr, v(GI), ALU.mult))
            link(V.tensor_tensor(v(T2), ci, v(GR), ALU.mult))
            link(V.tensor_tensor(v(TI), v(T1), v(T2), ALU.add))
            sre, sim = cs[:, K_S:K_S + 1], cs[:, K_S + 1:K_S + 2]
            link(V.tensor_scalar(v(T1), v(TI), sim, None, ALU.mult))
            link(V.scalar_tensor_tensor(out=v(PP), in0=v(TR_), scalar=sre, in1=v(T1), op0=ALU.mult, op1=ALU.subtract))
            link(V.tensor_scalar(v(T2), v(TR_), sim, None, ALU.mult))
            link(V.scalar_tensor_tensor(out=v(QQ), in0=v(TI), scalar=sre, in1=v(T2), op0=ALU.mult, op1=ALU.add))
            us3, uc3 = kk[:, 0:UCOLS].rearrange("p (h n) -> p h n", n=UN), kk[:, UCOLS:2 * UCOLS].rearrange("p (h n) -> p h n", n=UN)
            V.tensor_tensor(us3, xs[:, 0:UCOLS].rearrange("p (h n) -> p h n", n=UN),
                            v(QQ).unsqueeze(2).to_broadcast([P, C, UN]), ALU.mult)
            link(V.tensor_tensor(uc3, xs[:, X_COS:X_COS + UCOLS].rearrange("p (h n) -> p h n", n=UN),
                                 v(PP).unsqueeze(2).to_broadcast([P, C, UN]), ALU.mult))
            link(V.tensor_tensor(kk[:, 0:UCOLS], kk[:, UCOLS:2 * UCOLS], kk[:, 0:UCOLS], ALU.subtract))
            V.tensor_tensor(kk[:, 0:UCOLS], kk[:, 0:UCOLS], ex[:, 0:UCOLS], ALU.mult)
            V.tensor_tensor(xs[:, X_V:X_N], xs[:, X_V:X_N], ex[:, UCOLS:], ALU.mult).then_inc(s["kuv"], 1)
            dve.wait_ge(s["wms"], 1)
            V.tensor_tensor(wms[:, :, 1, :].bitcast(F32R), wmp.rearrange("c (s d) -> c s d", d=C),
                            wms[:, :, 0, :], ALU.subtract).then_inc(s["wms"], 1)
            dve.wait_ge(s["kps"], 1)
            for n in range(2):
                last = V.tensor_scalar(kf[:].rearrange("i h j -> i (h j)")[:, n * 512:(n + 1) * 512], kp[n], 2.0,
                                       None, ALU.mult)
            link(last)
            dve.wait_ge(s["small"], 48)
            d0 = kf[0:1, :, 0:1].rearrange("i h j -> i (h j)")
            V.tensor_tensor(d0, d0, dsk[:], ALU.add).then_inc(s["kf"], 1)
            dve.wait_ge(s["lens"], 16)
            link(V.tensor_copy(lenf[:], leni[:]))
            link(V.tensor_scalar(mk[:], tvals, lenf[:, 0:1], None, ALU.is_lt))

            def evac(it, first):
                def u_low(k):
                    dve.wait_ge(s["uhi"], it * 4 + k + 1)
                    V.tensor_tensor(us[1][:, k, :], ur[:, k, :], us[0][:, k, :].bitcast(F32),
                                    ALU.subtract).then_inc(s[f"usp{k}"], 1)

                def w_low(q):
                    dve.wait_ge(s["whi"], it * 3 + q + 1)
                    cols = bass.ds((it * 3 + q) * WC, WC)
                    V.tensor_tensor(wres[1][:, cols], wr[:, q, :], wres[0][:, cols].bitcast(F32),
                                    ALU.subtract).then_inc(s[f"wsp{q}"], 1)

                def out_of_psum(k):
                    dve.wait_ge(s[f"y{k}"], it + 1)
                    if not first:
                        dve.wait_ge(s[f"yst{k // 2}"], it * 16)
                    V.tensor_tensor(yo[:, k, :], yp[k], mk[:], ALU.mult).then_inc(s[f"ev{k}"], 1)

                u_low(1)
                w_low(0)
                out_of_psum(0)
                u_low(3)
                w_low(1)
                out_of_psum(1)
                w_low(2)
                out_of_psum(2)
                out_of_psum(3)

            evac(0, True)
            with dve.Fori(1, C // 4) as it:
                evac(it, False)
            dve.wait_ge(s["ev3"], C // 4)
            for q in range(3):
                dve.wait_ge(s[f"wsp{q}"], C // 4)
            for k in range(4):
                dve.wait_ge(s[f"usp{k}"], C // 4)
                dve.wait_ge(s[f"tsp{k}"], C // 4)
            dve.sem_inc(s["done"], 1)
            dve.wait_ge(s["done"], 3)
            dve.sem_inc(s["accD"], 1)

            def x3_lo(i):
                for g in range(NG):
                    dve.wait_ge(s["x3hi"], i * NG + g + 1)
                    V.tensor_tensor(x3s[1][:, :, g * P:(g + 1) * P], x3p[g].rearrange("p (k n) -> p k n", k=KT),
                                    x3s[0][:, :, g * P:(g + 1) * P].bitcast(F32), ALU.subtract
                                    ).then_inc(s["x3lo"], 1)

            def t_mask(i):
                dve.wait_ge(s["la"], i + 1)
                for g in range(NG):
                    for u in range(2):
                        o = (2 * g + u) * P
                        last = V.tensor_tensor(
                            tsb[:, o:o + P].rearrange("p (q r l) -> p q r l", q=GB, l=2),
                            la[:, g * P:(g + 1) * P].rearrange("p (q u r) -> p q u r", q=GB, u=2)[:, :, u, :]
                            .unsqueeze(3).to_broadcast([P, GB, RANK, 2]),
                            blk.rearrange("p (q r l) -> p q r l", q=GB, l=2), ALU.mult)
                last.then_inc(s["tm"], 1)

            def t_low(i):
                dve.wait_ge(s["th"], i + 1)
                V.tensor_tensor(th[1][:].rearrange("p g u n -> p (g u n)"), la,
                                th[0][:].rearrange("p g u n -> p (g u n)").bitcast(F32), ALU.subtract
                                ).then_inc(s["tl"], 1)

            def act_mul(i, j):
                m = P if j < FT - 1 else FTAIL
                dve.wait_ge(s["silu"], i * FT + j + 1)
                V.tensor_tensor(sg[0:m, j % 2, :], sg[0:m, j % 2, :], wk[j % 2][0:m, TB:2 * TB], ALU.mult
                                ).then_inc(s["mul"], 1)

            x3_lo(0)
            t_mask(0)
            t_low(0)
            act_mul(0, 0)

            def dve_block(i, last):
                for j in range(1, FT):
                    act_mul(i, j)
                if not last:
                    x3_lo(i + 1)
                dve.wait_ge(s["tdone"], i + 1)
                V.tensor_tensor(tdm[:].rearrange("p (g q w) -> p g q w", g=NG, q=GB),
                                tdp[:, 0:NG * P].rearrange("p (g q w) -> p g q w", g=NG, q=GB),
                                blk.rearrange("p (q w) -> p q w", q=GB).unsqueeze(1).to_broadcast(
                                    [P, NG, GB, 2 * RANK]), ALU.mult).then_inc(s["tdm"], 1)
                dve.wait_ge(s["tdm"], i + 1)
                tq = tdm[:].rearrange("p (q l r) -> p q l r", l=2, r=RANK)
                V.tensor_tensor(tdd[:].rearrange("p g (q r l) -> p (g q) r l", l=2, r=RANK),
                                tq[:, :, 0, :].unsqueeze(3).to_broadcast([P, NG * GB, RANK, 2]),
                                tq[:, :, 1, :].unsqueeze(3).to_broadcast([P, NG * GB, RANK, 2]), ALU.add
                                ).then_inc(s["tdd"], 1)
                if not last:
                    t_mask(i + 1)
                    t_low(i + 1)
                dve.wait_ge(s["tdth"], i + 1)
                V.tensor_tensor(tdt[1][:].rearrange("p g n -> p (g n)"), tdp[:, 256:512],
                                tdt[0][:].rearrange("p g n -> p (g n)").bitcast(F32), ALU.subtract
                                ).then_inc(s["tdtl"], 1)
                if not last:
                    act_mul(i + 1, 0)
                dve.wait_ge(s["accd"], i + 1)
                V.tensor_copy(io[:, 1, :], acc[1]).then_inc(s["accD"], 1)

            with dve.Fori(0, NBLK - 1) as i:
                dve_block(i, False)
            dve_block(NBLK - 1, True)

        @block.tensor
        def _(pe):
            mm = nc.tensor.matmul
            pe.wait_ge(s["kst"], 1)
            for c in range(NCOND):
                last = mm(wmp[:, c * C:(c + 1) * C], w1s[:, c, :], w2s[:, c, :], start=True, stop=True)
            last.then_inc(s["wm"], 1)
            pe.wait_ge(s["kuv"], 1)
            for h in range(C):
                n, o = h // (C // 2), h % (C // 2) * UI
                last = mm(kp[n][:, o:o + UI], kk[:, h * UN:(h + 1) * UN],
                          xs[:, X_V + h * UI:X_V + (h + 1) * UI], start=True, stop=True)
            last.then_inc(s["kps"], 1)
            PASSES = ((0, 0), (0, 1), (1, 0))

            def conv_block(it, first):
                for k in range(4):
                    pe.wait_ge(s[f"usp{k}"], it + 1)
                    pe.wait_ge(s[f"tsp{k}"], it + 1)
                    if not first:
                        pe.wait_ge(s[f"ev{k}"], it)
                    for c in range(KT):
                        for a, b in PASSES:
                            last = mm(yp[k][:, c * P:T], us[a][:, k, c * P:(c + 1) * P], ts_[b][:, k, 0:T - c * P],
                                      start=(c == 0 and a + b == 0), stop=(c == KT - 1 and a == 1))
                    last.then_inc(s[f"y{k}"], 1)

            conv_block(0, True)
            with pe.Fori(1, C // 4) as it:
                conv_block(it, False)
            pe.wait_ge(s["done"], 3)

            def mix_transposed(i):
                for g in range(NG):
                    for k in range(KT):
                        for a, b in PASSES:
                            last = mm(x3p[g][:, k * P:(k + 1) * P], x1s[a][:, g, k * P:(k + 1) * P],
                                      wbd[:, g, b, :], start=(a + b == 0), stop=(a == 1))
                    last.then_inc(s["x3mm"], 1)

            def lora_a(i):
                for g in range(NG):
                    for k in range(KT):
                        for a, b in PASSES:
                            w = ag[:, g * GB:(g + 1) * GB, b, :].rearrange("p q (u k r) -> p q u k r", u=2, k=KT)
                            last = mm(la[:, g * P:(g + 1) * P].rearrange("p (q u r) -> p q u r", q=GB, u=2),
                                      x3s[a][:, k, g * P:(g + 1) * P], w[:, :, :, k, :],
                                      start=(k == 0 and a + b == 0), stop=(k == KT - 1 and a == 1))
                last.then_inc(s["la"], 1)

            def lora_a_transposes(i):
                pe.wait_ge(s["tm"], i + 1)
                for q in range(2 * NG):
                    last = nc.tensor.transpose(la[:, q * P:(q + 1) * P], tsb[:, q * P:(q + 1) * P], ident)
                last.then_inc(s["tt"], 1)

            def gate_up(i, j):
                m = P if j < FT - 1 else FTAIL
                c = j // BJ
                for u in range(2):
                    o = wk[j % 2][0:m, u * TB:(u + 1) * TB]
                    for k in range(KT):
                        for a, b in PASSES:
                            mm(o, wgu[a][:, u, k, j * P:j * P + m], x3s[b][:, k, :],
                               start=(u == 0 and k == 0 and a + b == 0), stop=False, skip_group_check=True)
                    if j == 0 and u == 0:
                        lora_a_transposes(i)
                if j == 0:
                    pe.wait_ge(s["tl"], i + 1)
                if j % BJ == 0:
                    pe.wait_ge(s[f"b{c % 2}"], (i * (len(BCH) // 2) + c // 2 + 1) * 16 * BB)
                for u in range(2):
                    for g in range(NG):
                        for l in range(2):
                            last = mm(wk[j % 2][0:m, u * TB + g * P:u * TB + (g + 1) * P],
                                      bg[:, c % 2, g, j % BJ, u, 0:m], th[l][:, g, u, :],
                                      start=False, stop=(u == 1 and g == NG - 1 and l == 1), skip_group_check=True)
                last.then_inc(s["gu"], 1)

            def start_acc(i):
                for g in range(NG):
                    for n, (a, b) in enumerate(PASSES):
                        last = mm(acc[g], wbd[:, g, a, :], x1s[b][:, g, :], start=(n == 0), stop=False,
                                  skip_group_check=True)
                last.then_inc(s["accin"], 1)

            def down(i, j):
                m = P if j < FT - 1 else FTAIL
                adv = [adg[:, :, l, :].rearrange("p b (j r) -> p b j r", j=FT) for l in range(2)]
                for g in range(NG):
                    hi = ac[0][0:m, j % 2, g * P:(g + 1) * P]
                    lo = ac[1][0:m, j % 2, g * P:(g + 1) * P]
                    td3 = tdp[:, g * P:(g + 1) * P].rearrange("p (q l r) -> p q l r", q=GB, l=2)
                    adh = adg[0:m, g * GB:(g + 1) * GB, :, j * RANK:(j + 1) * RANK]
                    mm(acc[g], hi, wdn[0][0:m, j, :], start=False, stop=False, skip_group_check=True)
                    mm(acc[g], hi, wdn[1][0:m, j, :], start=False, stop=False, skip_group_check=True)
                    mm(td3, hi, adh, start=(j == 0 and g == 0), stop=False, skip_group_check=True)
                    mm(acc[g], lo, wdn[0][0:m, j, :], start=False, stop=False, skip_group_check=True)
                    last = mm(td3[:, :, 0, :], lo, adh[:, :, 0, :], start=False,
                              stop=(j == FT - 1 and g == NG - 1), skip_group_check=True)
                last.then_inc(s["tdone" if j == FT - 1 else "down"], 1)

            def lora_b_down(i):
                for g in range(NG):
                    for l in range(2):
                        last = mm(acc[g], tdt[l][:, g, :], bdg[:, g, :], start=False, stop=(l == 1),
                                  skip_group_check=True)
                last.then_inc(s["accd"], 1)

            def transposes(i):
                for g in range(NG):
                    last = nc.tensor.transpose(tdp[:, (NG + g) * P:(NG + g + 1) * P], tdd[:, g, :], ident)
                last.then_inc(s["tdx"], 1)

            def next_mix(i):
                pe.wait_ge(s["x1lo"], i * NG + NG)
                pe.wait_ge(s["wbd"], (i + 1) * 16 * BB)
                mix_transposed(i)

            next_mix(0)
            pe.wait_ge(s["x3lo"], NG)
            pe.wait_ge(s["ag"], 16 * BB)
            lora_a(0)
            gate_up(0, 0)

            def pe_block(i, last):
                for j in range(1, FT):
                    if j >= 2:
                        pe.wait_ge(s["mul"], i * FT + j - 1)
                    gate_up(i, j)
                    if j == 1:
                        pe.wait_ge(s["accA"], i + 1)
                        pe.wait_ge(s["accD"], i + 1)
                        start_acc(i)
                        pe.wait_ge(s["adg"], (i + 1) * 16 * BB)
                    pe.wait_ge(s["alo"], i * FT + j)
                    down(i, j - 1)
                    if j == MIXJ and not last:
                        next_mix(i + 1)
                pe.wait_ge(s["alo"], i * FT + FT)
                down(i, FT - 1)
                if not last:
                    pe.wait_ge(s["x3lo"], i * NG + 2 * NG)
                    pe.wait_ge(s["ag"], (i + 2) * 16 * BB)
                    lora_a(i + 1)
                pe.wait_ge(s["tdd"], i + 1)
                transposes(i)
                if not last:
                    pe.wait_ge(s["mul"], i * FT + FT)
                    gate_up(i + 1, 0)
                pe.wait_ge(s["tdtl"], i + 1)
                pe.wait_ge(s["bdg"], (i + 1) * 16 * BB)
                lora_b_down(i)

            with pe.Fori(0, NBLK - 1) as i:
                pe_block(i, False)
            pe_block(NBLK - 1, True)


def kernel(**inputs):
    import numpy as np
    import concourse.bacc as bacc
    from concourse import mybir as mb
    from concourse.bass_utils import run_bass_kernel_spmd

    g = {k: np.ascontiguousarray(v) for k, v in inputs.items()}
    x = g["x"]
    xT = x.transpose(1, 2, 0).reshape(C, KT, P, B)[:, :, ::-1].transpose(0, 2, 1, 3).reshape(C, P, KT * B)

    def twice(a):
        return np.concatenate([a.T, a.T], axis=0)

    ssm = np.stack([twice(g["L0_cond_log_A_real"]), twice(g["L0_cond_A_imag"]), twice(g["L0_cond_C"][..., 0]),
                    twice(g["L0_cond_C"][..., 1]), np.broadcast_to(g["L0_cond_log_dt"], (P, C))], axis=1)
    cst = np.zeros((P, K_N), np.float32)
    cst[:, K_ID:K_ID + P] = np.eye(P)
    cst[:, K_BLK:K_BLK + P] = 0.5 * np.kron(np.eye(GB), np.ones((C, C)))
    cst[:, K_T:K_T + T] = np.arange(T)
    cst[:, K_PU:K_PU + UN] = UI * np.arange(UN)
    cst[:, K_PV:K_PV + UI] = np.arange(UI)
    cst[:NS, K_S] = 1.0
    cst[NS:, K_S + 1] = 1.0
    cst[:NS, K_S + 2] = 0.25
    cst[:NS, K_S + 3] = np.pi / 2
    cst[:, K_S + 4] = np.pi / 2
    cst[:, K_S + 5] = PIC - cst[:, K_S + 3]
    cst[:, K_S + 6] = -PIC - cst[:, K_S + 3]

    def hidden(w):
        o = np.zeros((P, KT, FP), np.float32)
        o[:, :, :F] = w.T.reshape(KT, P, F).transpose(1, 0, 2)
        return o.reshape(P, KT * FP)

    wd = np.zeros((FP, T), np.float32)
    wd[:F] = g["L3_cond_W_down"].T
    wall = np.concatenate([hidden(g["L3_cond_W_gate"]), hidden(g["L3_cond_W_up"]),
                           wd.reshape(FT, P, T).transpose(1, 0, 2).reshape(P, FT * T)], axis=1)
    a2 = np.stack([g["L3_cond_A_gate"][0], g["L3_cond_A_up"][0]], axis=1)
    ta = a2.reshape(NA, 2, RANK, KT, P).transpose(4, 0, 1, 3, 2).reshape(P, NA, WA)
    ad = np.zeros((NA, RANK, FP), np.float32)
    ad[:, :, :F] = g["L3_cond_A_down"][0]
    tad = ad.reshape(NA, RANK, FT, P).transpose(3, 0, 2, 1).reshape(P, NA, WAD)
    b2 = np.zeros((NA, RANK, 2, FP), np.float32)
    b2[:, :, 0, :F] = g["L3_cond_B_gate"][0].transpose(0, 2, 1)
    b2[:, :, 1, :F] = g["L3_cond_B_up"][0].transpose(0, 2, 1)
    tb = b2.reshape(NA, RANK, 2, FT, P).transpose(0, 1, 3, 2, 4).reshape(2, P, WB).transpose(1, 0, 2)
    tbd = g["L3_cond_B_down"][0].transpose(0, 2, 1).reshape(2, P, WBD).transpose(1, 0, 2)

    arrays = {
        "xT": xT, "x": x.reshape(B * C, T), "lens": g["itok_B_78_3631"].reshape(B, 1),
        "cidx": g["itok_B_0_15"].reshape(1, B), "lidx": g["itok_B_2_6"].reshape(1, B), "ssm": ssm,
        "dskip": g["L0_cond_D"].reshape(1, C), "cst": cst, "w1t": g["L1_cond_weights"].transpose(2, 0, 1),
        "w2": g["L2_cond_weights"].transpose(1, 0, 2), "wall": wall, "ta": ta, "tad": tad, "tb": tb, "tbd": tbd,
    }
    nc = bacc.Bacc("TRN2", target_bir_lowering=False, num_devices=1)
    feeds, args = {}, []
    for name, a in arrays.items():
        a = np.ascontiguousarray(a)
        feeds["in_" + name] = a
        args.append(nc.dram_tensor("in_" + name, a.shape, mb.dt.from_np(a.dtype), kind="ExternalInput").ap())
    args.append(nc.dram_tensor("out_x", (B * C, T), mb.dt.from_np(np.dtype("float32")), kind="ExternalOutput").ap())
    cond_resid_kernel(nc, *args)
    r = run_bass_kernel_spmd(nc, [feeds], core_ids=[0])
    return r.results[0]["out_x"].reshape(B, C, T)
```

```python
import math
from contextlib import ExitStack

import concourse.bass as bass
from concourse import mybir

ALU = mybir.AluOpType
ACT = mybir.ActivationFunctionType
F32 = mybir.dt.float32
F32R = mybir.dt.float32r
I32 = mybir.dt.int32
SP, ACTE = mybir.EngineType.SP, mybir.EngineType.Activation

B, C, T = 128, 32, 512
NS = 64
NCOND = 16
F = 1376
NA, RANK = 16, 16
P = 128
KT = T // P
FT = -(-F // P)
FTAIL = F - (FT - 1) * P
FP = FT * P
UI, UN = 32, T // 32
GB = P // C
NG = 2
BB = NG * GB
TB = BB * C
NBLK = B // BB
WGU = 2 * KT * FP
WCOLS = WGU + FT * T
NWC = 8
WC = WCOLS // NWC
NW0 = 1
NWP = 4
BJ = 2
BCH = [list(range(j, min(j + BJ, FT))) for j in range(0, FT, BJ)]
WA, WAD, WB, WBD = RANK * 2 * KT, RANK * FT, FT * 2 * P, T
XJ = (4, 7)
WBDJ = {1: (0, 1), 2: (2, 3), 3: (4, 5), 4: (6, 7)}
AGJ = {6: (0, 1, 2), 7: (3, 4, 5), 8: (6, 7)}
AGSJ = 9
BDJ = 5
CHJ = {2 * c - 1: c for c in range(2, len(BCH))}
MIXJ = (6, 9)
RESJ = 1
ROUND = 12582912.0
PIC = 3.1415925
C1 = 6.28125
C2 = 2.0 * math.pi - C1
L1 = 0.693359375
L2 = math.log(2.0) - L1
K_ID, K_BLK = 0, 128
K_N = 384
K_T, K_PU, K_PV, K_S = 0, 512, 528, 560
K_PN = 568
UCOLS, VCOLS = C * UN, C * UI
X_SB = UCOLS
X_SBH = UCOLS + C
X_COS = UCOLS + 2 * C
X_CB = X_COS + UCOLS
X_V = X_CB + C
X_N = X_V + VCOLS


def cond_resid_kernel(nc, xT, x, lens, idx, ssm, dskip, cst, cstp, w1t, w2, wall, ta, tad, tb, tbd, out):
    kpad = nc.dram_tensor("kpad", (C, P + T), F32, kind="Internal").ap()
    x1p = nc.dram_tensor("x1p", (B * C, T), F32, kind="Internal").ap()
    tm_d = nc.dram_tensor("tm_d", (NCOND, C, 2, C), F32, kind="Internal").ap()
    x1p_bct = x1p.rearrange("(b c) t -> b c t", c=C)

    ctx = ExitStack()
    with ctx:
        def sem(name):
            return ctx.enter_context(nc.semaphore(name))

        def sbin(stack):
            return lambda name, shape, dt=F32: stack.enter_context(nc.sbuf_tensor(name, shape, dt))

        ps = ctx.enter_context(nc.psum_tensor("ps", [P, 8, 512], F32))
        acc = [ps[:, g, :] for g in range(NG)]
        x3p = [ps[:, 2 + g, :] for g in range(NG)]
        wk = [ps[:, 4 + n, :] for n in range(2)]
        la = ps[:, 6, :]
        tdp = ps[:, 7, 0:TB]
        yp = [ps[:, n, :] for n in range(4)]
        kp = [ps[0:UN, 6 + n, :] for n in range(2)]
        wmp = ps[0:C, 5, :]

        def split_buffers(name, shape):
            hi = sbin(ctx)(name + "_hi", shape, F32R)
            with ExitStack() as raw_only:
                raw = sbin(raw_only)(name + "_raw", shape)
            return hi, raw, sbin(ctx)(name + "_lo", shape, F32R)

        sb = sbin(ctx)
        cs = sb("cs", [P, K_N])
        ixs = sb("ixs", [1, 2 * B], I32)
        leni = sb("leni", [P, 1], I32)
        lenf = sb("lenf", [P, 1])
        w_hi, w_raw, w_lo = split_buffers("w", [P, WCOLS])
        wres = [w_hi[:], w_lo[:]]
        conv = ExitStack()
        prep = ExitStack()
        sb = sbin(prep)
        csp = sb("csp", [P, K_PN])
        pk = sb("pk", [P, 5, C])
        dsk = sb("dsk", [1, C])
        xs = sb("xs", [P, X_N])
        kk = sb("kk", [P, X_N])
        ex = sb("ex", [P, UCOLS + VCOLS])
        sm = sb("sm", [P, 24, C])
        two_k = sb("two_k", [P, 2, C], I32)
        zer = sb("zer", [C, P])
        kf = sb("kf", [UN, C, UI])
        wms = sb("wms", [C, NCOND, 2, C])
        w1s = sb("w1s", [C, NCOND, C])
        w2s = sb("w2s", [C, NCOND, C])
        prep.close()
        sb = sbin(conv)
        us = [sb("us_hi", [P, 4, KT * B], F32R), sb("us_lo", [P, 4, KT * B], F32R)]
        ts_ = [sb("ts_hi", [P, 4, T], F32R), sb("ts_lo", [P, 4, T], F32R)]
        yo = sb("yo", [P, 4, T])
        tr = sb("tr", [P, 4, T])
        ur = sb("ur", [P, 4, KT * B])
        mk = sb("mk", [P, T])
        conv.close()
        sb = sbin(ctx)
        adg_hi, adg_raw, adg_lo = split_buffers("adg", [P, BB * WAD])
        bg_hi, bg_raw, bg_lo = split_buffers("bg", [P, 2, BJ * 2 * P])
        bdg_hi, bdg_raw, bdg_lo = split_buffers("bdg", [P, WBD])
        x1s = [sb("x1_hi", [P, T], F32R), sb("x1_lo", [P, T], F32R)]
        x3n = sb("x3n", [P, NG, T])
        xres = sb("xres", [P, NG, T])
        x3s = [sb("x3_hi", [P, KT, TB], F32R), sb("x3_lo", [P, KT, TB], F32R)]
        tsb = sb("tsb", [P, 2, TB])
        th = [sb("t_hi", [P, 2, TB], F32R), sb("t_lo", [P, 2, TB], F32R)]
        sg = sb("sg", [P, 2, TB])
        ac = [sb("act_hi", [P, 2, TB], F32R), sb("act_lo", [P, 2, TB], F32R)]
        tdm = sb("tdm", [P, TB])
        tdt = [sb("tdt_hi", [P, TB], F32R), sb("tdt_lo", [P, TB], F32R)]
        ag_hi, ag_raw, ag_lo = split_buffers("ag", [P, BB * WA])
        io = sb("io", [P, 2, T])
        wbd = sb("wbd", [P, NG, 2, P], F32R)

        names = """pk cst cstp small lens w12 zer kf kst kout wm wms tst u0 u1 tt0 tt1
            a1 da dch ph ex tg kuv kps uhi thi usp0 usp1 usp2 usp3 tsp0 tsp1 tsp2 tsp3 whi wlo wlv y0 y1 y2 y3
            ev0 ev1 ev2 ev3 yst0 yst1 done ag aghi aglo adg adhi adlo b0 b1 bhi blo bdg bdhi bdlo wbd
            xin xr xsum x1hi x1lo x3mm x3n x3t res x3hi x3lo la tm th tl gu silu mul ahi alo down
            tdone tdm tdth tdtl accd evac ost wz""".split() + [f"wl{n}" for n in range(NWC)]
        s = {n: sem("s_" + n) for n in names}

        def at(eng, value):
            return value if isinstance(value, int) else eng.snap(value)

        wgu = [w[:, 0:WGU].rearrange("p (u k f) -> p u k f", u=2, k=KT) for w in wres]
        wdn = [w[:, WGU:WCOLS].rearrange("p (j t) -> p j t", j=FT) for w in wres]
        ident = cs[:, K_ID:K_ID + P]
        blk = cs[:, K_BLK:K_BLK + TB]
        tvals = csp[:, K_T:K_T + T]

        def load_toeplitz(eng, h, p):
            src = kpad[bass.ds(h, 2), 0:T] if not isinstance(h, int) else kpad[h:h + 2, 0:T]
            src = bass.AP(src.tensor, src.offset, [[1, P], [P + T, 2], [1, T]])
            eng.dma_start(tr[:, 2 * p:2 * p + 2, :], src).then_inc(s[f"tt{p}"], 16)

        def rows_of(b):
            return b // GB, (b % GB) * C, (b % GB + 1) * C

        def entries(engine, i, which, count):
            row = ixs[0:1, bass.ds((i * 2 + which) * BB, BB)]
            _, values = nc.values_load_multi_w_load_instructions(row, engines=(engine,), min_val=0, max_val=count - 1)
            return [bass.ds(v, 1) for v in values]

        def load_ag(eng, e, batches):
            for b in batches:
                eng.dma_start(ag_raw[:, b * WA:(b + 1) * WA], ta[e[b]].rearrange("a p w -> (a p) w")
                              ).then_inc(s["ag"], 16)

        def load_wbd(eng, e, batches):
            for b in batches:
                g, p0, p1 = rows_of(b)
                eng.dma_start(wbd[p0:p1, g, :, p0:p1].bitcast(F32), tm_d[e[b]].rearrange("a c l d -> (a c) l d")
                              ).then_inc(s["wbd"], 16)

        pu = csp[:, K_PU:K_PU + UN]
        pv = csp[:, K_PV:K_PV + UI]

        def outer(eng, dst, col, powers, n):
            return eng.tensor_tensor(dst.rearrange("p (h n) -> p h n", n=n),
                                     sm[:, col, :].unsqueeze(2).to_broadcast([P, C, n]),
                                     powers.unsqueeze(1).to_broadcast([P, C, n]), ALU.mult)

        def w_cols(n):
            return slice(n * WC, (n + 1) * WC)

        block = ctx.enter_context(nc.Block())

        @block.sync
        def _(sp):
            sp.dma_start(pk[:], ssm).then_inc(s["pk"], 16)
            sp.dma_start(csp[:], cstp).then_inc(s["cstp"], 16)
            sp.dma_start(cs[:], cst).then_inc(s["cst"], 16)
            sp.dma_start(w1s[:], w1t).then_inc(s["w12"], 16)
            sp.dma_start(w2s[:], w2).then_inc(s["w12"], 16)
            sp.dma_start(dsk[:], dskip).then_inc(s["small"], 16)
            sp.dma_start(leni[:], lens).then_inc(s["lens"], 16)
            sp.dma_start(ixs[:], idx).then_inc(s["small"], 16)
            for p in range(2):
                sp.dma_start(ur[:, 2 * p:2 * p + 2, :], xT[2 * p:2 * p + 2].rearrange("c p w -> p c w")
                             ).then_inc(s[f"u{p}"], 16)
            for n in range(NWC - 1):
                sp.dma_start(w_raw[:, w_cols(n)], wall[:, w_cols(n)]).then_inc(s[f"wl{n}"], 16)
            sp.wait_ge(s["wms"], 2)
            sp.dma_start(tm_d.rearrange("s c l d -> c s l d"), wms[:]).then_inc(s["tst"], 16)
            sp.wait_ge(s["small"], 32)
            first_mixes, first_adapters = entries(SP, 0, 1, NCOND), entries(SP, 0, 0, NA)
            sp.wait_ge(s["wz"], 1)
            sp.wait_ge(s["tst"], 16)
            load_wbd(sp, first_mixes, range(BB))

            def conv_io(it, first, last):
                nxt = [at(sp, it * 4 + 4 + 2 * p) for p in range(2)]
                here = [at(sp, it * 4 + 2 * p) for p in range(2)]

                def load_u(p):
                    sp.wait_ge(s[f"usp{2 * p}"], it + 1)
                    sp.wait_ge(s[f"usp{2 * p + 1}"], it + 1)
                    sp.dma_start(ur[:, 2 * p:2 * p + 2, :],
                                 xT[bass.ds(nxt[p], 2)].rearrange("c p w -> p c w")).then_inc(s[f"u{p}"], 16)

                if first:
                    load_u(0)
                    load_u(1)
                    load_ag(sp, first_adapters, range(BB))
                    sp.dma_start(io[:, 1, :], x[0:P, :]).then_inc(s["xin"], 16)
                for p in range(2):
                    if not last:
                        if not first:
                            load_u(p)
                        sp.wait_ge(s[f"tsp{2 * p}"], it + 1)
                        sp.wait_ge(s[f"tsp{2 * p + 1}"], it + 1)
                        load_toeplitz(sp, nxt[p], p)
                    sp.wait_ge(s[f"ev{2 * p}"], it + 1)
                    sp.wait_ge(s[f"ev{2 * p + 1}"], it + 1)
                    sp.dma_start(x1p_bct[:, bass.ds(here[p], 2), :], yo[:, 2 * p:2 * p + 2, :]
                                 ).then_inc(s[f"yst{p}"], 16)

            conv_io(0, True, False)
            with sp.Fori(1, C // 4 - 1) as it:
                conv_io(it, False, False)
            conv_io(C // 4 - 1, False, True)
            sp.wait_ge(s["yst0"], 16 * C // 4)
            sp.wait_ge(s["yst1"], 16 * C // 4)
            sp.dma_start(io[:, 0, :], x1p[0:P, :]).then_inc(s["xin"], 16)
            sp.wait_ge(s["done"], 3)

            def load_adg(e, free):
                if free is not None:
                    sp.wait_ge(*free)
                for b in range(BB):
                    sp.dma_start(adg_raw[:, b * WAD:(b + 1) * WAD], tad[e[b]].rearrange("a p w -> (a p) w")
                                 ).then_inc(s["adg"], 16)

            def load_b(e, c, free):
                if free is not None:
                    sp.wait_ge(*free)
                o, w = BCH[c][0] * 2 * P, len(BCH[c]) * 2 * P
                for b in range(BB):
                    sp.dma_start(bg_raw[b * RANK:(b + 1) * RANK, c % 2, 0:w],
                                 tb[e[b], :, o:o + w].rearrange("a k w -> (a k) w")).then_inc(s[f"b{c % 2}"], 16)

            def load_bdg(e, free):
                if free is not None:
                    sp.wait_ge(*free)
                for b in range(BB):
                    sp.dma_start(bdg_raw[b * RANK:(b + 1) * RANK, :], tbd[e[b]].rearrange("a k w -> (a k) w")
                                 ).then_inc(s["bdg"], 16)

            def load_x(i, g, stored=None):
                first = at(sp, i * TB + g * P)
                if stored is not None:
                    sp.wait_ge(s["ost"], stored)
                if g > 0:
                    sp.wait_ge(s["x1lo"], i * NG + g)
                sp.dma_start(io[:, 0, :], x1p[bass.ds(first, P), :]).then_inc(s["xin"], 16)
                sp.dma_start(io[:, 1, :], x[bass.ds(first, P), :]).then_inc(s["xin"], 16)

            def store_out(i):
                first = [at(sp, i * TB + g * P) for g in range(NG)]
                for g in range(NG):
                    sp.wait_ge(s["evac"], (i + 1) * NG + g + 1)
                    sp.dma_start(out[bass.ds(first[g], P), :], io[:, g, :]).then_inc(s["ost"], 16)

            def block_io(i, first, last):
                e = entries(SP, i, 0, NA)
                if first:
                    sp.dma_start(xres[:, 0, :], x1p[P:2 * P, :]).then_inc(s["xr"], 16)
                    sp.dma_start(xres[:, 1, :], x[P:2 * P, :]).then_inc(s["xr"], 16)
                load_b(e, 0, None if first else (s["gu"], (i - 1) * FT + BCH[-2][-1] + 1))
                load_b(e, 1, None if first else (s["gu"], i * FT))
                load_adg(e, None if first else (s["tdone"], i))
                load_bdg(e, None if first else (s["accd"], i))
                if not first:
                    store_out(i - 1)
                for c in range(2, len(BCH)):
                    load_b(e, c, (s["gu"], i * FT + BCH[c - 2][-1] + 1))
                    if c < 4 and not last:
                        load_x(i + 1, c - 2, i * 16 * NG if c == 2 and not first else None)

            block_io(0, True, False)
            with sp.Fori(1, NBLK - 1) as i:
                block_io(i, False, False)
            block_io(NBLK - 1, False, True)
            store_out(NBLK - 1)
            sp.wait_ge(s["ost"], 16 * NG * NBLK)

        @block.gpsimd
        def _(pool):
            nc.gpsimd.memset(zer[:], 0.0).then_inc(s["zer"], 1)
            nc.gpsimd.memset(wbd[:].bitcast(F32), 0.0).then_inc(s["wz"], 1)
            pool.wait_ge(s["da"], 1)
            pool.wait_ge(s["cstp"], 16)
            outer(nc.gpsimd, ex[:, 0:UCOLS], 2, pu, UN)
            outer(nc.gpsimd, ex[:, UCOLS:], 2, pv, UI).then_inc(s["ex"], 1)
            pool.wait_ge(s["w12"], 32)
            pool.wait_ge(s["cst"], 16)
            idc = cs[0:C, K_ID:K_ID + C].unsqueeze(1).to_broadcast([C, NCOND, C])
            nc.gpsimd.tensor_tensor(w1s[:], w1s[:], idc, ALU.add).then_inc(s["kst"], 1)
            nc.gpsimd.tensor_tensor(w2s[:], w2s[:], idc, ALU.add).then_inc(s["kst"], 1)

            def w_low(n):
                pool.wait_ge(s["whi"], n + 1)
                nc.gpsimd.tensor_tensor(w_lo[:, w_cols(n)], w_raw[:, w_cols(n)], w_hi[:, w_cols(n)].bitcast(F32),
                                        ALU.subtract).then_inc(s["wlo"], 1)

            w_low(0)
            pool.wait_ge(s["tg"], 1)
            nc.gpsimd.tensor_tensor(xs[:, X_V:X_N], xs[:, X_V:X_N], ex[:, UCOLS:], ALU.mult).then_inc(s["kuv"], 1)
            for n in range(1, NWP):
                w_low(n)

            def lows(it):
                for k in range(4):
                    pool.wait_ge(s["thi"], it * 4 + k + 1)
                    nc.gpsimd.tensor_tensor(ts_[1][:, k, :], tr[:, k, :], ts_[0][:, k, :].bitcast(F32),
                                            ALU.subtract).then_inc(s[f"tsp{k}"], 1)

            with pool.Fori(0, C // 4) as it:
                lows(it)
            for k in range(4):
                pool.wait_ge(s[f"tsp{k}"], C // 4)
            pool.wait_ge(s["yst0"], 16 * C // 4)
            pool.wait_ge(s["yst1"], 16 * C // 4)
            pool.sem_inc(s["done"], 1)
            pool.wait_ge(s["done"], 3)

            def block_sum(i, g):
                pool.wait_ge(s["xin"], (i * NG + g) * 32)
                nc.gpsimd.tensor_tensor(io[:, 0, :], io[:, 0, :], io[:, 1, :], ALU.add).then_inc(s["xsum"], 1)
                pool.wait_ge(s["x1hi"], i * NG + g + 1)
                nc.gpsimd.tensor_tensor(x1s[1][:], io[:, 0, :], x1s[0][:].bitcast(F32),
                                        ALU.subtract).then_inc(s["x1lo"], 1)

            def ag_low(i):
                pool.wait_ge(s["aghi"], i + 1)
                nc.gpsimd.tensor_tensor(ag_lo[:], ag_raw[:], ag_hi[:].bitcast(F32), ALU.subtract
                                        ).then_inc(s["aglo"], 1)

            def bdg_low(i):
                pool.wait_ge(s["bdhi"], i + 1)
                nc.gpsimd.tensor_tensor(bdg_lo[:], bdg_raw[:], bdg_hi[:].bitcast(F32), ALU.subtract
                                        ).then_inc(s["bdlo"], 1)

            ag_low(0)
            for n in range(NWP + 2, NWC):
                w_low(n)

            def lows3(i, last):
                for j in range(FT):
                    m = P if j < FT - 1 else FTAIL
                    pool.wait_ge(s["ahi"], i * FT + j + 1)
                    nc.gpsimd.tensor_tensor(ac[1][0:m, j % 2, :], sg[0:m, j % 2, :], ac[0][0:m, j % 2, :].bitcast(F32),
                                            ALU.subtract).then_inc(s["alo"], 1)
                    if j in XJ and not last:
                        block_sum(i + 1, XJ.index(j))
                    if j == BDJ:
                        bdg_low(i)
                    if j == AGSJ and not last:
                        ag_low(i + 1)

            with pool.Fori(0, NBLK - 1) as i:
                lows3(i, False)
            lows3(NBLK - 1, True)

        @block.scalar
        def _(act):
            def w_high(chunks):
                for n in chunks:
                    act.wait_ge(s[f"wl{n}"], 16)
                    nc.scalar.activation(w_hi[:, w_cols(n)], w_raw[:, w_cols(n)], ACT.Copy).then_inc(s["whi"], 1)

            act.wait_ge(s["zer"], 1)
            act.dma_start(kpad[:, 0:P - 1], zer[:, 0:P - 1]).then_inc(s["kout"], 16)
            act.wait_ge(s["ex"], 1)
            nc.scalar.activation(sm[:, 4, :], sm[:, 2, :], ACT.Tanh, scale=0.5).then_inc(s["a1"], 1)
            nc.scalar.activation(ex[:], ex[:], ACT.Exp).then_inc(s["a1"], 1)
            w_high(range(0, NW0))
            act.wait_ge(s["ph"], 1)
            for lo, hi, off in ((0, X_COS, None), (X_COS, X_V, K_S + 4), (X_V, X_N, K_S + 3)):
                last = nc.scalar.activation(xs[:, lo:hi], xs[:, lo:hi], ACT.Sin,
                                            **({} if off is None else {"bias": csp[:, off:off + 1]}))
            last.then_inc(s["tg"], 1)
            act.wait_ge(s["wm"], 1)
            wm3 = wmp.rearrange("c (s d) -> c s d", d=C)
            nc.scalar.activation(wms[:, :, 0, :].bitcast(F32R), wm3, ACT.Copy).then_inc(s["wms"], 1)
            w_high(range(NW0, NWC - 1))
            act.wait_ge(s["kf"], 1)
            act.dma_start(kpad[:, P - 1:P - 1 + T].rearrange("h (i j) -> i h j", j=UI), kf[:]).then_inc(s["kout"], 16)
            for k in range(4):
                act.wait_ge(s[f"u{k // 2}"], 16)
                nc.scalar.activation(us[0][:, k, :], ur[:, k, :], ACT.Copy).then_inc(s["uhi"], 1)
            act.wait_ge(s["kout"], 32)
            act.wait_ge(s["tst"], 16)
            for p in range(2):
                load_toeplitz(act, 2 * p, p)
            act.dma_start(w_raw[:, w_cols(NWC - 1)], wall[:, w_cols(NWC - 1)]).then_inc(s[f"wl{NWC - 1}"], 16)

            def highs(it, first):
                for k in range(4):
                    if not first:
                        act.wait_ge(s[f"u{k // 2}"], it * 16 + 16)
                        act.wait_ge(s[f"y{k}"], it)
                        nc.scalar.activation(us[0][:, k, :], ur[:, k, :], ACT.Copy).then_inc(s["uhi"], 1)
                    act.wait_ge(s[f"tt{k // 2}"], it * 16 + 16)
                    nc.scalar.activation(ts_[0][:, k, :], tr[:, k, :], ACT.Copy).then_inc(s["thi"], 1)

            highs(0, True)
            w_high((NWC - 1,))
            with act.Fori(1, C // 4) as it:
                highs(it, False)
            for k in range(4):
                act.wait_ge(s[f"y{k}"], C // 4)
            act.sem_inc(s["done"], 1)
            act.wait_ge(s["done"], 3)

            def x1_hi(i, g, first=False, xin=io):
                act.wait_ge(s["xsum"], i * NG + g + 1)
                if not first:
                    act.wait_ge(s["x3mm"], i * NG + g)
                nc.scalar.activation(x1s[0][:], xin[:, 0, :], ACT.Copy).then_inc(s["x1hi"], 1)

            def x3_copy(i, g, first=False):
                act.wait_ge(s["x3mm"], i * NG + g + 1)
                if not first:
                    act.wait_ge(s["res"], i)
                nc.scalar.activation(x3n[:, g, :], x3p[g], ACT.Copy).then_inc(s["x3n"], 1)

            def residual(i):
                act.wait_ge(s["evac"], (i + 1) * NG)
                nc.scalar.activation(xres[:], x3n[:], ACT.Copy).then_inc(s["res"], 1)

            def ag_hi_(i):
                act.wait_ge(s["ag"], (i + 1) * 16 * BB)
                nc.scalar.activation(ag_hi[:], ag_raw[:], ACT.Copy).then_inc(s["aghi"], 1)

            def adg_hi_(i):
                act.wait_ge(s["adg"], (i + 1) * 16 * BB)
                nc.scalar.activation(adg_hi[:], adg_raw[:], ACT.Copy).then_inc(s["adhi"], 1)

            def bdg_hi_(i):
                act.wait_ge(s["bdg"], (i + 1) * 16 * BB)
                nc.scalar.activation(bdg_hi[:], bdg_raw[:], ACT.Copy).then_inc(s["bdhi"], 1)

            def b_hi(i, c):
                w = len(BCH[c]) * 2 * P
                act.wait_ge(s[f"b{c % 2}"], (i * (len(BCH) // 2) + c // 2 + 1) * 16 * BB)
                nc.scalar.activation(bg_hi[:, c % 2, 0:w], bg_raw[:, c % 2, 0:w], ACT.Copy).then_inc(s["bhi"], 1)

            def x3_hi(i):
                for g in range(NG):
                    act.wait_ge(s["x3t"], i * NG + g + 1)
                    nc.scalar.activation(x3s[0][:, :, g * P:(g + 1) * P],
                                         x3p[g].rearrange("p (k n) -> p k n", k=KT), ACT.Copy).then_inc(s["x3hi"], 1)

            def t_hi(i):
                act.wait_ge(s["tm"], i + 1)
                nc.scalar.activation(th[0][:], tsb[:], ACT.Copy).then_inc(s["th"], 1)

            def act_tile(i, j):
                m = P if j < FT - 1 else FTAIL
                act.wait_ge(s["gu"], i * FT + j + 1)
                nc.scalar.activation(sg[0:m, j % 2, :], wk[j % 2][0:m, 0:TB], ACT.Silu).then_inc(s["silu"], 1)
                act.wait_ge(s["mul"], i * FT + j + 1)
                nc.scalar.activation(ac[0][0:m, j % 2, :], sg[0:m, j % 2, :], ACT.Copy).then_inc(s["ahi"], 1)

            ag_hi_(0)
            x1_hi(0, 0, True)
            x3_copy(0, 0, True)
            x1_hi(0, 1, xin=xres)
            x3_copy(0, 1, True)
            x3_hi(0)
            b_hi(0, 0)
            t_hi(0)
            act_tile(0, 0)
            b_hi(0, 1)
            adg_hi_(0)

            def act_block(i, last):
                for j in range(1, FT):
                    act_tile(i, j)
                    if j in CHJ:
                        b_hi(i, CHJ[j])
                    if j == RESJ:
                        residual(i)
                    if j == BDJ:
                        bdg_hi_(i)
                    if last:
                        continue
                    if j == 1:
                        conds = entries(ACTE, i + 1, 1, NCOND)
                    if j == 4:
                        adapters = entries(ACTE, i + 1, 0, NA)
                    if j in WBDJ:
                        load_wbd(act, conds, WBDJ[j])
                    if j in AGJ:
                        load_ag(act, adapters, AGJ[j])
                    if j in XJ:
                        x1_hi(i + 1, XJ.index(j))
                    if j in MIXJ:
                        x3_copy(i + 1, MIXJ.index(j))
                    if j == AGSJ:
                        ag_hi_(i + 1)
                if not last:
                    x3_hi(i + 1)
                    b_hi(i + 1, 0)
                    t_hi(i + 1)
                act.wait_ge(s["tdm"], i + 1)
                nc.scalar.activation(tdt[0][:], tdm[:], ACT.Copy).then_inc(s["tdth"], 1)
                if not last:
                    act_tile(i + 1, 0)
                    b_hi(i + 1, 1)
                if not last:
                    adg_hi_(i + 1)

            with act.Fori(0, NBLK - 1) as i:
                act_block(i, False)
            act_block(NBLK - 1, True)

        @block.vector
        def _(dve):
            chain = [0]

            def link(ins):
                chain[0] += 1
                ins.then_inc(s["dch"], 1)
                dve.wait_ge(s["dch"], chain[0])

            V = nc.vector

            def w_low(n):
                dve.wait_ge(s["whi"], n + 1)
                V.tensor_tensor(w_lo[:, w_cols(n)], w_raw[:, w_cols(n)], w_hi[:, w_cols(n)].bitcast(F32),
                                ALU.subtract).then_inc(s["wlv"], 1)


            def v(n):
                return sm[:, n, :]

            DT, EA, A_, BI, TH = 0, 1, 2, 3, 4
            aim, cr, ci = pk[:, 2, :], pk[:, 3, :], pk[:, 4, :]
            dve.wait_ge(s["pk"], 16)
            ek, er, eq, e0 = sm[:, 5:7, :], sm[:, 7:9, :], sm[:, 9:11, :], sm[:, 11:13, :]
            link(V.tensor_scalar(e0, pk[:, 0:2, :], 87.0, -87.0, ALU.min, ALU.max))
            link(V.tensor_scalar(ek, e0, 1.0 / math.log(2.0), ROUND, ALU.mult, ALU.add))
            link(V.tensor_scalar(ek, ek, -ROUND, None, ALU.add))
            link(V.scalar_tensor_tensor(out=er, in0=ek, scalar=-L1, in1=e0, op0=ALU.mult, op1=ALU.add))
            V.tensor_scalar(two_k[:], ek, 127.0, 2.0 ** 23, ALU.add, ALU.mult)
            link(V.scalar_tensor_tensor(out=er, in0=ek, scalar=-L2, in1=er, op0=ALU.mult, op1=ALU.add))
            link(V.tensor_scalar(eq, er, 1.0 / 5040.0, None, ALU.mult))
            for n in range(6, 0, -1):
                link(V.scalar_tensor_tensor(out=eq, in0=eq, scalar=1.0 / math.factorial(n), in1=er, op0=ALU.add,
                                            op1=ALU.mult))
            link(V.scalar_tensor_tensor(out=sm[:, 0:2, :], in0=eq, scalar=1.0, in1=two_k[:].bitcast(F32),
                                        op0=ALU.add, op1=ALU.mult))
            V.scalar_tensor_tensor(out=v(A_), in0=v(EA), scalar=-1.0, in1=v(DT), op0=ALU.mult, op1=ALU.mult
                                   ).then_inc(s["da"], 1)
            link(V.tensor_tensor(v(BI), aim, v(DT), ALU.mult))
            dve.wait_ge(s["cstp"], 16)
            outer(V, xs[:, 0:UCOLS], BI, pu, UN)
            outer(V, xs[:, X_COS:X_COS + UCOLS], BI, pu, UN)
            outer(V, xs[:, X_V:X_N], BI, pv, UI)
            V.tensor_copy(xs[:, X_SB:X_SB + C], v(BI))
            V.tensor_copy(xs[:, X_CB:X_CB + C], v(BI))
            link(V.tensor_scalar(xs[:, X_SBH:X_SBH + C], v(BI), 0.5, None, ALU.mult))
            i2p = 1.0 / (2.0 * math.pi)
            col = [csp[:, K_S + n:K_S + n + 1] for n in range(8)]
            parts = ((0, X_COS, 0.0, PIC, -PIC), (X_COS, X_V, 0.25, PIC - math.pi / 2, -PIC - math.pi / 2),
                     (X_V, X_N, col[2], col[5], col[6]))
            for lo, hi, turn, _, _ in parts:
                last = V.tensor_scalar(kk[:, lo:hi], xs[:, lo:hi], i2p, turn, ALU.mult, ALU.add)
            link(last)
            link(V.tensor_scalar(kk[:], kk[:], ROUND, -ROUND, ALU.add, ALU.add))
            for c in (C1, C2):
                link(V.scalar_tensor_tensor(out=xs[:], in0=kk[:], scalar=-c, in1=xs[:], op0=ALU.mult, op1=ALU.add))
            for lo, hi, _, top, bottom in parts:
                last = V.tensor_scalar(xs[:, lo:hi], xs[:, lo:hi], top, bottom, ALU.min, ALU.max)
            last.then_inc(s["ph"], 1)
            dve.wait_ge(s["lens"], 16)
            link(V.tensor_copy(lenf[:], leni[:]))
            link(V.tensor_scalar(mk[:], tvals, lenf[:, 0:1], None, ALU.is_lt))
            dve.wait_ge(s["a1"], 2)
            OM, RC, EM, A2, I2, ER, EI, GR, GI, TR_, TI = 5, 6, 7, 8, 9, 10, 11, 12, 13, 14, 15
            T1, T2, PP, QQ, XA, XB = 16, 17, 18, 19, 20, 22
            def pair(n):
                return sm[:, n:n + 2, :]

            def twice(a):
                return a.unsqueeze(1).to_broadcast([P, 2, C])

            V.tensor_tensor(v(A2), v(EA), v(EA), ALU.mult)
            V.tensor_tensor(v(T1), aim, aim, ALU.mult)
            link(V.tensor_scalar(v(OM), v(TH), -1.0, 1.0, ALU.mult, ALU.add))
            V.tensor_tensor(v(A2), v(A2), v(T1), ALU.add)
            link(V.reciprocal(v(RC), v(OM)))
            V.reciprocal(v(I2), v(A2))
            link(V.scalar_tensor_tensor(out=v(EM), in0=v(TH), scalar=2.0, in1=v(RC), op0=ALU.mult, op1=ALU.mult))
            dve.wait_ge(s["tg"], 1)
            sb_, cb, sbh = xs[:, X_SB:X_SB + C], xs[:, X_CB:X_CB + C], xs[:, X_SBH:X_SBH + C]
            V.tensor_tensor(v(T1), sbh, sbh, ALU.mult)
            V.scalar_tensor_tensor(out=v(EI), in0=v(EM), scalar=1.0, in1=sb_, op0=ALU.add, op1=ALU.mult)
            link(V.tensor_tensor(v(ER), v(EM), cb, ALU.mult))
            link(V.scalar_tensor_tensor(out=v(ER), in0=v(T1), scalar=-2.0, in1=v(ER), op0=ALU.mult, op1=ALU.add))
            V.tensor_tensor(pair(XA), pair(ER), twice(aim), ALU.mult)
            link(V.tensor_tensor(pair(XB), pair(ER), twice(v(EA)), ALU.mult))
            V.tensor_tensor(v(GR), v(XA + 1), v(XB), ALU.subtract)
            link(V.scalar_tensor_tensor(out=v(GI), in0=v(XB + 1), scalar=-1.0, in1=v(XA), op0=ALU.mult,
                                        op1=ALU.subtract))
            link(V.tensor_tensor(pair(GR), pair(GR), twice(v(I2)), ALU.mult))
            V.tensor_tensor(pair(XA), pair(GR), twice(cr), ALU.mult)
            link(V.tensor_tensor(pair(XB), pair(GR), twice(ci), ALU.mult))
            V.tensor_tensor(v(TR_), v(XA), v(XB + 1), ALU.subtract)
            link(V.tensor_tensor(v(TI), v(XA + 1), v(XB), ALU.add))
            sre, sim = csp[:, K_S:K_S + 1], csp[:, K_S + 1:K_S + 2]
            V.tensor_scalar(v(T1), v(TI), sim, None, ALU.mult)
            link(V.tensor_scalar(v(T2), v(TR_), sim, None, ALU.mult))
            V.scalar_tensor_tensor(out=v(PP), in0=v(TR_), scalar=sre, in1=v(T1), op0=ALU.mult, op1=ALU.subtract)
            link(V.scalar_tensor_tensor(out=v(QQ), in0=v(TI), scalar=sre, in1=v(T2), op0=ALU.mult, op1=ALU.add))
            us3 = kk[:, 0:UCOLS].rearrange("p (h n) -> p h n", n=UN)
            uc3 = kk[:, UCOLS:2 * UCOLS].rearrange("p (h n) -> p h n", n=UN)
            V.tensor_tensor(us3, xs[:, 0:UCOLS].rearrange("p (h n) -> p h n", n=UN),
                            v(QQ).unsqueeze(2).to_broadcast([P, C, UN]), ALU.mult)
            link(V.tensor_tensor(uc3, xs[:, X_COS:X_COS + UCOLS].rearrange("p (h n) -> p h n", n=UN),
                                 v(PP).unsqueeze(2).to_broadcast([P, C, UN]), ALU.mult))
            link(V.tensor_tensor(kk[:, 0:UCOLS], kk[:, UCOLS:2 * UCOLS], kk[:, 0:UCOLS], ALU.subtract))
            V.tensor_tensor(kk[:, 0:UCOLS], kk[:, 0:UCOLS], ex[:, 0:UCOLS], ALU.mult).then_inc(s["kuv"], 1)
            dve.wait_ge(s["wms"], 1)
            V.tensor_tensor(wms[:, :, 1, :].bitcast(F32R), wmp.rearrange("c (s d) -> c s d", d=C),
                            wms[:, :, 0, :], ALU.subtract).then_inc(s["wms"], 1)
            for n in range(2):
                dve.wait_ge(s["kps"], n + 1)
                last = V.tensor_scalar(kf[:].rearrange("i h j -> i (h j)")[:, n * 512:(n + 1) * 512], kp[n], 2.0,
                                       None, ALU.mult)
            link(last)
            dve.wait_ge(s["small"], 32)
            d0 = kf[0:1, :, 0:1].rearrange("i h j -> i (h j)")
            V.tensor_tensor(d0, d0, dsk[:], ALU.add).then_inc(s["kf"], 1)

            w_low(NWP)

            def evac(it, first):
                def u_low(k):
                    dve.wait_ge(s["uhi"], it * 4 + k + 1)
                    V.tensor_tensor(us[1][:, k, :], ur[:, k, :], us[0][:, k, :].bitcast(F32),
                                    ALU.subtract).then_inc(s[f"usp{k}"], 1)

                def out_of_psum(k):
                    dve.wait_ge(s[f"y{k}"], it + 1)
                    if not first:
                        dve.wait_ge(s[f"yst{k // 2}"], it * 16)
                    V.tensor_tensor(yo[:, k, :], yp[k], mk[:], ALU.mult).then_inc(s[f"ev{k}"], 1)

                if first:
                    for k in range(4):
                        u_low(k)
                    w_low(NWP + 1)
                    out_of_psum(0)
                else:
                    u_low(0)
                    u_low(1)
                    u_low(2)
                    out_of_psum(0)
                    u_low(3)
                out_of_psum(1)
                out_of_psum(2)
                out_of_psum(3)

            evac(0, True)
            with dve.Fori(1, C // 4) as it:
                evac(it, False)
            dve.wait_ge(s["ev3"], C // 4)
            for k in range(4):
                dve.wait_ge(s[f"usp{k}"], C // 4)
            dve.sem_inc(s["done"], 1)
            dve.wait_ge(s["done"], 3)
            dve.sem_inc(s["evac"], NG)

            def x3_lo(i):
                for g in range(NG):
                    dve.wait_ge(s["x3hi"], i * NG + g + 1)
                    V.tensor_tensor(x3s[1][:, :, g * P:(g + 1) * P], x3p[g].rearrange("p (k n) -> p k n", k=KT),
                                    x3s[0][:, :, g * P:(g + 1) * P].bitcast(F32), ALU.subtract
                                    ).then_inc(s["x3lo"], 1)

            def t_mask(i):
                dve.wait_ge(s["la"], i + 1)
                V.tensor_tensor(tsb[:], la.rearrange("p (u n) -> p u n", u=2),
                                blk.unsqueeze(1).to_broadcast([P, 2, TB]), ALU.mult).then_inc(s["tm"], 1)

            def t_low(i):
                dve.wait_ge(s["th"], i + 1)
                V.tensor_tensor(th[1][:], tsb[:], th[0][:].bitcast(F32), ALU.subtract).then_inc(s["tl"], 1)

            def b_low(i, c):
                w = len(BCH[c]) * 2 * P
                dve.wait_ge(s["bhi"], i * len(BCH) + c + 1)
                V.tensor_tensor(bg_lo[:, c % 2, 0:w], bg_raw[:, c % 2, 0:w],
                                bg_hi[:, c % 2, 0:w].bitcast(F32), ALU.subtract).then_inc(s["blo"], 1)

            def adg_low(i):
                dve.wait_ge(s["adhi"], i + 1)
                V.tensor_tensor(adg_lo[:], adg_raw[:], adg_hi[:].bitcast(F32), ALU.subtract
                                ).then_inc(s["adlo"], 1)

            def act_mul(i, j):
                m = P if j < FT - 1 else FTAIL
                dve.wait_ge(s["silu"], i * FT + j + 1)
                V.tensor_tensor(sg[0:m, j % 2, :], sg[0:m, j % 2, :], wk[j % 2][0:m, TB:2 * TB], ALU.mult
                                ).then_inc(s["mul"], 1)

            for g, (xin, loaded) in enumerate(((io, "xin"), (xres, "xr"))):
                dve.wait_ge(s[loaded], 32)
                V.tensor_tensor(xin[:, 0, :], xin[:, 0, :], xin[:, 1, :], ALU.add).then_inc(s["xsum"], 1)
                dve.wait_ge(s["x1hi"], g + 1)
                V.tensor_tensor(x1s[1][:], xin[:, 0, :], x1s[0][:].bitcast(F32), ALU.subtract).then_inc(s["x1lo"], 1)
            x3_lo(0)
            b_low(0, 0)
            t_mask(0)
            t_low(0)
            act_mul(0, 0)
            b_low(0, 1)
            adg_low(0)

            def dve_block(i, last):
                for j in range(1, FT):
                    act_mul(i, j)
                    if j in CHJ:
                        b_low(i, CHJ[j])
                if not last:
                    x3_lo(i + 1)
                    b_low(i + 1, 0)
                dve.wait_ge(s["tdone"], i + 1)
                V.tensor_tensor(tdm[:], tdp, blk, ALU.mult).then_inc(s["tdm"], 1)
                if not last:
                    t_mask(i + 1)
                    t_low(i + 1)
                dve.wait_ge(s["tdth"], i + 1)
                V.tensor_tensor(tdt[1][:], tdm[:], tdt[0][:].bitcast(F32), ALU.subtract).then_inc(s["tdtl"], 1)
                if not last:
                    act_mul(i + 1, 0)
                    b_low(i + 1, 1)
                dve.wait_ge(s["accd"], i + 1)
                dve.wait_ge(s["res"], i + 1)
                for g in range(NG):
                    V.tensor_tensor(io[:, g, :], acc[g], xres[:, g, :], ALU.add).then_inc(s["evac"], 1)
                if not last:
                    adg_low(i + 1)

            with dve.Fori(0, NBLK - 1) as i:
                dve_block(i, False)
            dve_block(NBLK - 1, True)

        @block.tensor
        def _(pe):
            mm = nc.tensor.matmul
            pe.wait_ge(s["kst"], 2)
            for c in range(NCOND):
                last = mm(wmp[:, c * C:(c + 1) * C], w1s[:, c, :], w2s[:, c, :], start=True, stop=True)
            last.then_inc(s["wm"], 1)
            pe.wait_ge(s["kuv"], 2)
            for h in range(C):
                n, o = h // (C // 2), h % (C // 2) * UI
                last = mm(kp[n][:, o:o + UI], kk[:, h * UN:(h + 1) * UN],
                          xs[:, X_V + h * UI:X_V + (h + 1) * UI], start=True, stop=True)
                if (h + 1) % (C // 2) == 0:
                    last.then_inc(s["kps"], 1)
            PASSES = ((0, 0), (0, 1), (1, 0))

            def conv_block(it, first):
                for k in range(4):
                    pe.wait_ge(s[f"usp{k}"], it + 1)
                    pe.wait_ge(s[f"tsp{k}"], it + 1)
                    if not first:
                        pe.wait_ge(s[f"ev{k}"], it)
                    for c in range(KT):
                        for a, b in PASSES:
                            last = mm(yp[k][:, c * P:T], us[a][:, k, c * P:(c + 1) * P], ts_[b][:, k, 0:T - c * P],
                                      start=(c == 0 and a + b == 0), stop=(c == KT - 1 and a == 1))
                    last.then_inc(s[f"y{k}"], 1)

            conv_block(0, True)
            with pe.Fori(1, C // 4) as it:
                conv_block(it, False)

            def mix(i, g):
                pe.wait_ge(s["x1lo"], i * NG + g + 1)
                pe.wait_ge(s["wbd"], (i + 1) * 16 * BB)
                for n, (a, b) in enumerate(PASSES):
                    last = mm(x3p[g], wbd[:, g, a, :], x1s[b][:], start=(n == 0), stop=(n == 2))
                last.then_inc(s["x3mm"], 1)

            def transposes(i, g):
                pe.wait_ge(s["x3n"], i * NG + g + 1)
                for k in range(KT):
                    last = nc.tensor.transpose(x3p[g][:, k * P:(k + 1) * P], x3n[:, g, k * P:(k + 1) * P], ident)
                last.then_inc(s["x3t"], 1)

            def lora_a(i):
                for u in range(2):
                    for k in range(KT):
                        for a, b in PASSES:
                            w = (ag_hi[:], ag_lo[:])[a].rearrange("p (n w) -> p n w", w=2 * KT)[:, :, u * KT + k]
                            last = mm(la[:, u * TB:(u + 1) * TB], w, x3s[b][:, k, :],
                                      start=(u == 0 and k == 0 and a + b == 0), stop=(k == KT - 1 and a == 1),
                                      skip_group_check=True)
                last.then_inc(s["la"], 1)

            def gate_up(i, j):
                m = P if j < FT - 1 else FTAIL
                c = j // BJ
                out_ = [wk[j % 2][0:m, u * TB:(u + 1) * TB] for u in range(2)]
                for u in range(2):
                    for k in range(KT):
                        for a, b in PASSES:
                            mm(out_[u], wgu[a][:, u, k, j * P:j * P + m], x3s[b][:, k, :],
                               start=(u == 0 and k == 0 and a + b == 0), stop=False, skip_group_check=True)
                if j == 0:
                    pe.wait_ge(s["tl"], i + 1)
                if j % BJ == 0:
                    pe.wait_ge(s["blo"], i * len(BCH) + c + 1)
                for u in range(2):
                    for a, b in PASSES:
                        o = (j % BJ * 2 + u) * P
                        rows = (bg_hi[:, c % 2, o:o + m], bg_lo[:, c % 2, o:o + m])[a]
                        last = mm(out_[u], rows, th[b][:, u, :],
                                  start=False, stop=(u == 1 and a == 1), skip_group_check=True)
                last.then_inc(s["gu"], 1)

            def down(i, j):
                m = P if j < FT - 1 else FTAIL
                act_ = [ac[n][0:m, j % 2, :] for n in range(2)]
                adv = [a.rearrange("p (n j) -> p n j", j=FT)[:, :, j]
                       for a in (adg_hi[0:m, :], adg_lo[0:m, :])]

                def project(a, b):
                    for g in range(NG):
                        mm(acc[g], act_[a][:, g * P:(g + 1) * P], wdn[b][0:m, j, :],
                           start=(j == 0 and a + b == 0), stop=False, skip_group_check=True)

                project(0, 0)
                project(0, 1)
                pe.wait_ge(s["alo"], i * FT + j + 1)
                project(1, 0)
                if j == 0:
                    pe.wait_ge(s["adlo"], i + 1)
                for a, b in PASSES:
                    last = mm(tdp, adv[a], act_[b], start=(j == 0 and a + b == 0),
                              stop=(j == FT - 1 and a == 1), skip_group_check=True)
                last.then_inc(s["tdone" if j == FT - 1 else "down"], 1)

            def lora_b_down(i):
                for g in range(NG):
                    for a, b in PASSES:
                        rows = (bdg_hi[:], bdg_lo[:])[b]
                        last = mm(acc[g], tdt[a][:, g * P:(g + 1) * P], rows, start=False, stop=(a == 1),
                                  skip_group_check=True)
                last.then_inc(s["accd"], 1)

            for g in range(NG):
                mix(0, g)
                transposes(0, g)
            pe.wait_ge(s["x3lo"], NG)
            pe.wait_ge(s["aglo"], 1)
            lora_a(0)
            pe.wait_ge(s["wlo"], NWP)
            pe.wait_ge(s["wlv"], 2)
            gate_up(0, 0)
            pe.wait_ge(s["wlo"], NWC - 2)

            def pe_block(i, last):
                for j in range(1, FT):
                    if j >= 2:
                        pe.wait_ge(s["mul"], i * FT + j - 1)
                    gate_up(i, j)
                    if j == 1:
                        pe.wait_ge(s["evac"], (i + 1) * NG)
                    if j - 1 in MIXJ and not last:
                        transposes(i + 1, MIXJ.index(j - 1))
                    pe.wait_ge(s["ahi"], i * FT + j)
                    down(i, j - 1)
                    if j in MIXJ and not last:
                        mix(i + 1, MIXJ.index(j))
                pe.wait_ge(s["ahi"], i * FT + FT)
                down(i, FT - 1)
                if not last:
                    pe.wait_ge(s["x3lo"], i * NG + 2 * NG)
                    pe.wait_ge(s["aglo"], i + 2)
                    lora_a(i + 1)
                if not last:
                    pe.wait_ge(s["mul"], i * FT + FT)
                    gate_up(i + 1, 0)
                pe.wait_ge(s["tdtl"], i + 1)
                pe.wait_ge(s["bdlo"], i + 1)
                lora_b_down(i)

            with pe.Fori(0, NBLK - 1) as i:
                pe_block(i, False)
            pe_block(NBLK - 1, True)


def kernel(**inputs):
    import numpy as np
    import concourse.bacc as bacc
    from concourse import mybir as mb
    from concourse.bass_utils import run_bass_kernel_spmd

    g = {k: np.ascontiguousarray(v) for k, v in inputs.items()}
    x = g["x"]
    xT = x.transpose(1, 2, 0).reshape(C, KT, P, B)[:, :, ::-1].transpose(0, 2, 1, 3).reshape(C, P, KT * B)

    def twice(a):
        return np.concatenate([a.T, a.T], axis=0)

    ssm = np.stack([np.broadcast_to(g["L0_cond_log_dt"], (P, C)), twice(g["L0_cond_log_A_real"]),
                    twice(g["L0_cond_A_imag"]), twice(g["L0_cond_C"][..., 0]), twice(g["L0_cond_C"][..., 1])], axis=1)
    cst = np.zeros((P, K_N), np.float32)
    cst[:, K_ID:K_ID + P] = np.eye(P)
    cst[:, K_BLK:K_BLK + TB] = 0.5 * np.kron(np.eye(BB), np.ones((RANK, C)))
    cstp = np.zeros((P, K_PN), np.float32)
    cstp[:, K_T:K_T + T] = np.arange(T)
    cstp[:, K_PU:K_PU + UN] = UI * np.arange(UN)
    cstp[:, K_PV:K_PV + UI] = np.arange(UI)
    cstp[:NS, K_S] = 1.0
    cstp[NS:, K_S + 1] = 1.0
    cstp[:NS, K_S + 2] = 0.25
    cstp[:NS, K_S + 3] = np.pi / 2
    cstp[:, K_S + 4] = np.pi / 2
    cstp[:, K_S + 5] = PIC - cstp[:, K_S + 3]
    cstp[:, K_S + 6] = -PIC - cstp[:, K_S + 3]

    def hidden(w):
        o = np.zeros((P, KT, FP), np.float32)
        o[:, :, :F] = w.T.reshape(KT, P, F).transpose(1, 0, 2)
        return o.reshape(P, KT * FP)

    wd = np.zeros((FP, T), np.float32)
    wd[:F] = g["L3_cond_W_down"].T
    wall = np.concatenate([hidden(g["L3_cond_W_gate"]), hidden(g["L3_cond_W_up"]),
                           wd.reshape(FT, P, T).transpose(1, 0, 2).reshape(P, FT * T)], axis=1)
    a2 = np.stack([g["L3_cond_A_gate"][0], g["L3_cond_A_up"][0]], axis=1)
    ta = a2.reshape(NA, 2, RANK, KT, P).transpose(0, 4, 2, 1, 3).reshape(NA, P, WA)
    ad = np.zeros((NA, RANK, FP), np.float32)
    ad[:, :, :F] = g["L3_cond_A_down"][0]
    tad = ad.reshape(NA, RANK, FT, P).transpose(0, 3, 1, 2).reshape(NA, P, WAD)
    b2 = np.zeros((NA, RANK, 2, FP), np.float32)
    b2[:, :, 0, :F] = g["L3_cond_B_gate"][0].transpose(0, 2, 1)
    b2[:, :, 1, :F] = g["L3_cond_B_up"][0].transpose(0, 2, 1)
    tb = b2.reshape(NA, RANK, 2, FT, P).transpose(0, 1, 3, 2, 4).reshape(NA, RANK, WB)
    tbd = g["L3_cond_B_down"][0].transpose(0, 2, 1)

    arrays = {
        "xT": xT, "x": x.reshape(B * C, T), "lens": g["itok_B_78_3631"].reshape(B, 1),
        "idx": np.stack([g["itok_B_2_6"].reshape(NBLK, BB), g["itok_B_0_15"].reshape(NBLK, BB)],
                        axis=1).reshape(1, 2 * B),
        "ssm": ssm,
        "dskip": g["L0_cond_D"].reshape(1, C), "cst": cst, "cstp": cstp, "w1t": g["L1_cond_weights"].transpose(2, 0, 1),
        "w2": g["L2_cond_weights"].transpose(1, 0, 2), "wall": wall, "ta": ta, "tad": tad, "tb": tb, "tbd": tbd,
    }
    nc = bacc.Bacc("TRN2", target_bir_lowering=False, num_devices=1)
    feeds, args = {}, []
    for name, a in arrays.items():
        a = np.ascontiguousarray(a)
        feeds["in_" + name] = a
        args.append(nc.dram_tensor("in_" + name, a.shape, mb.dt.from_np(a.dtype), kind="ExternalInput").ap())
    args.append(nc.dram_tensor("out_x", (B * C, T), mb.dt.from_np(np.dtype("float32")), kind="ExternalOutput").ap())
    cond_resid_kernel(nc, *args)
    r = run_bass_kernel_spmd(nc, [feeds], core_ids=[0])
    return r.results[0]["out_x"].reshape(B, C, T)
```
